# Optimizing a Trainium2 kernel written in Bass

```python
import numpy as np
import jax
import jax.numpy as jnp

def _softmax(x, axis=-1):
    return jax.nn.softmax(x, axis=axis)

def _gelu(x):
    return jax.nn.gelu(x, approximate=True)

def _silu(x):
    return jax.nn.silu(x)

def _sigmoid(x):
    return jax.nn.sigmoid(x)

def _layernorm(x, axis=-1, eps=1e-05):
    m = jnp.mean(x, axis=axis, keepdims=True)
    v = jnp.var(x, axis=axis, keepdims=True)
    return (x - m) / jnp.sqrt(v + eps)

def _scatter_add(tgt, idx, src, axis=0):
    return tgt.at[idx].add(src)

def _segment_sum(src, seg, n):
    return jax.ops.segment_sum(src, seg, n)
kernel_name = 'mk_early_fusion_embed_d1_tok_img1024_r4_210c10'

def setup_inputs(seed: int=0):
    np.random.seed(seed)
    _w = jnp.asarray

    def _rec_inputs():
        import jax
        import jax.numpy as jnp
        _rk = jax.random.key(seed)
        x = 0.00021031 + 1.00007 * jax.random.normal(jax.random.fold_in(_rk, 1), (16, 1, 256, 256), jnp.float32)
        x_txt = jax.random.randint(jax.random.fold_in(_rk, 51), (16, 77), 0, 12564, jnp.int32)
        return (x, x_txt)
    x, x_txt = _rec_inputs()

    def _L0_tok_setup():
        import jax, jax.numpy as jnp
        import numpy as np
        KERNEL = jnp.array([[[[1.0, 0.0], [0.0, -1.0]]], [[[0.0, -1.0], [1.0, 0.0]]]], dtype=jnp.float32)
        key = jax.random.key(seed)
        images = jax.random.normal(key, (32, 1, 256, 256), dtype=jnp.float32)
        return {'images': images}
    _L0_tok_all = _L0_tok_setup()
    _L0_tok_in = {k: v for k, v in _L0_tok_all.items() if k in ()}
    del _L0_tok_all

    def _L0_txt_setup():
        import jax, jax.numpy as jnp
        import numpy as np
        VOCAB = 50257
        DIM = 256
        PADDING_IDX = 0
        key = jax.random.key(seed)
        k_w, k_ids = jax.random.split(key)
        weight = jax.random.normal(k_w, (VOCAB, DIM), dtype=jnp.float32)
        weight = weight.at[PADDING_IDX].set(0.0)
        input_ids = jax.random.randint(k_ids, (16, 512), 0, VOCAB, dtype=jnp.int64)
        return {'weight': weight, 'input_ids': input_ids}
    _L0_txt_all = _L0_txt_setup()
    _L0_txt_in = {k: v for k, v in _L0_txt_all.items() if k in ('weight',)}
    del _L0_txt_all

    def _L0_attn_setup():
        import jax, jax.numpy as jnp
        import numpy as np
        import math
        B, S, HID = (2, 1000, 256)
        H, W, STRIDE = (16, 128, 64)
        D = HID // H
        key = jax.random.key(seed)
        ks = jax.random.split(key, 10)
        std = 0.02
        inp = {'hidden_states': jax.random.normal(ks[0], (B, S, HID), dtype=jnp.float32), 'Wq': jax.random.normal(ks[1], (HID, HID), dtype=jnp.float32) * std, 'bq': jnp.zeros((HID,), dtype=jnp.float32), 'Wk': jax.random.normal(ks[2], (HID, HID), dtype=jnp.float32) * std, 'bk': jnp.zeros((HID,), dtype=jnp.float32), 'Wv': jax.random.normal(ks[3], (HID, HID), dtype=jnp.float32) * std, 'bv': jnp.zeros((HID,), dtype=jnp.float32), 'Wo': jax.random.normal(ks[4], (HID, HID), dtype=jnp.float32) * std, 'bo': jnp.zeros((HID,), dtype=jnp.float32), 'pos_bias': jax.random.normal(ks[5], (H, W, W), dtype=jnp.float32) * std}
        return inp
    _L0_attn_all = _L0_attn_setup()
    _L0_attn_in = {k: v for k, v in _L0_attn_all.items() if k in ('Wq', 'bq', 'Wk', 'bk', 'Wv', 'bv', 'Wo', 'bo', 'pos_bias')}
    del _L0_attn_all

    def _L0_ffn_setup():
        import jax, jax.numpy as jnp
        import numpy as np
        E, K, D, H = (8, 2, 256, 512)
        B, S = (1, 256)

        def _grouped_swiglu(x_sorted, counts, w1, w2, w3):
            if hasattr(jax.lax, 'ragged_dot'):
                gs = counts.astype(jnp.int32)
                h = jax.nn.silu(jax.lax.ragged_dot(x_sorted, w1, gs)) * jax.lax.ragged_dot(x_sorted, w3, gs)
                return jax.lax.ragged_dot(h, w2, gs)
            pos = jnp.arange(x_sorted.shape[0])
            eid = jnp.searchsorted(jnp.cumsum(counts), pos, side='right')
            out = jnp.zeros((x_sorted.shape[0], w2.shape[-1]), x_sorted.dtype)
            for e in range(w1.shape[0]):
                xm = jnp.where((eid == e)[:, None], x_sorted, 0.0)
                he = jax.nn.silu(xm @ w1[e]) * (xm @ w3[e])
                out = out + he @ w2[e]
            return out
        key = jax.random.key(seed)
        k0, k1, k2, k3, k4 = jax.random.split(key, 5)
        sD = 1.0 / np.sqrt(D)
        sH = 1.0 / np.sqrt(H)
        return {'hidden_states': jax.random.normal(k0, (B, S, D), jnp.float32), 'gate_w': jax.random.normal(k1, (E, D), jnp.float32) * sD, 'w1': jax.random.normal(k2, (E, D, H), jnp.float32) * sD, 'w2': jax.random.normal(k3, (E, H, D), jnp.float32) * sH, 'w3': jax.random.normal(k4, (E, D, H), jnp.float32) * sD}
    _L0_ffn_all = _L0_ffn_setup()
    _L0_ffn_in = {k: v for k, v in _L0_ffn_all.items() if k in ('gate_w', 'w1', 'w2', 'w3')}
    del _L0_ffn_all
    return {'x': x, 'x_txt': x_txt, 'L0_txt_weight': _L0_txt_in['weight'], 'L0_attn_Wq': _L0_attn_in['Wq'], 'L0_attn_bq': _L0_attn_in['bq'], 'L0_attn_Wk': _L0_attn_in['Wk'], 'L0_attn_bk': _L0_attn_in['bk'], 'L0_attn_Wv': _L0_attn_in['Wv'], 'L0_attn_bv': _L0_attn_in['bv'], 'L0_attn_Wo': _L0_attn_in['Wo'], 'L0_attn_bo': _L0_attn_in['bo'], 'L0_attn_pos_bias': _L0_attn_in['pos_bias'], 'L0_ffn_gate_w': _L0_ffn_in['gate_w'], 'L0_ffn_w1': _L0_ffn_in['w1'], 'L0_ffn_w2': _L0_ffn_in['w2'], 'L0_ffn_w3': _L0_ffn_in['w3']}

def reference(x, x_txt, L0_txt_weight, L0_attn_Wq, L0_attn_bq, L0_attn_Wk, L0_attn_bk, L0_attn_Wv, L0_attn_bv, L0_attn_Wo, L0_attn_bo, L0_attn_pos_bias, L0_ffn_gate_w, L0_ffn_w1, L0_ffn_w2, L0_ffn_w3):
    import jax
    import jax.numpy as jnp

    def _L0_tok_ref(images):
        import jax, jax.numpy as jnp
        import numpy as np
        KERNEL = jnp.array([[[[1.0, 0.0], [0.0, -1.0]]], [[[0.0, -1.0], [1.0, 0.0]]]], dtype=jnp.float32)
        out = jax.lax.conv_general_dilated(images, KERNEL, window_strides=(1, 1), padding=((0, 1), (0, 1)), dimension_numbers=('NCHW', 'OIHW', 'NCHW'))
        return jnp.clip(jnp.sum(jnp.abs(out), axis=1), 0.0, 1.0)

    def _L0_txt_ref(weight, input_ids):
        import jax, jax.numpy as jnp
        import numpy as np
        VOCAB = 50257
        DIM = 256
        PADDING_IDX = 0
        return jnp.take(weight, input_ids, axis=0)

    def _L0_attn_ref(hidden_states, Wq, bq, Wk, bk, Wv, bv, Wo, bo, pos_bias):
        import jax, jax.numpy as jnp
        import numpy as np
        import math
        B, S, HID = (2, 1000, 256)
        H, W, STRIDE = (16, 128, 64)
        D = HID // H
        Bb, Ss, Hid = hidden_states.shape
        scale = 1.0 / math.sqrt(D)

        def split_heads(x):
            return x.reshape(Bb, Ss, H, D).transpose(0, 2, 1, 3)
        q = split_heads(hidden_states @ Wq + bq)
        k = split_heads(hidden_states @ Wk + bk)
        v = split_heads(hidden_states @ Wv + bv)
        n_win = (Ss - W) // STRIDE + 1
        starts = jnp.arange(n_win) * STRIDE
        idx = starts[:, None] + jnp.arange(W)
        qw = q[:, :, idx]
        kw = k[:, :, idx]
        vw = v[:, :, idx]
        scores = jnp.einsum('bhnqd,bhnkd->bhnqk', qw, kw) * scale + pos_bias[None, :, None]
        probs = jax.nn.softmax(scores, axis=-1)
        ow = jnp.einsum('bhnqk,bhnkd->bhnqd', probs, vw)
        flat = idx.reshape(-1)
        merged = jnp.zeros((Bb, H, Ss, D), dtype=ow.dtype).at[:, :, flat].add(ow.reshape(Bb, H, -1, D))
        counts = jnp.zeros((Ss,), dtype=jnp.float32).at[flat].add(1.0)
        ls = Ss - W
        qt, kt, vt = (q[:, :, ls:], k[:, :, ls:], v[:, :, ls:])
        st = jnp.einsum('bhqd,bhkd->bhqk', qt, kt) * scale + pos_bias[None]
        ot = jnp.einsum('bhqk,bhkd->bhqd', jax.nn.softmax(st, axis=-1), vt)
        merged = merged.at[:, :, ls:].add(ot)
        counts = counts.at[ls:].add(1.0)
        merged = merged / jnp.clip(counts, 1.0, None)[None, None, :, None]
        ctx = merged.transpose(0, 2, 1, 3).reshape(Bb, Ss, Hid)
        return ctx @ Wo + bo

    def _L0_ffn_ref(hidden_states, gate_w, w1, w2, w3):
        import jax, jax.numpy as jnp
        import numpy as np
        E, K, D, H = (8, 2, 256, 512)
        B, S = (1, 256)

        def _grouped_swiglu(x_sorted, counts, w1, w2, w3):
            if hasattr(jax.lax, 'ragged_dot'):
                gs = counts.astype(jnp.int32)
                h = jax.nn.silu(jax.lax.ragged_dot(x_sorted, w1, gs)) * jax.lax.ragged_dot(x_sorted, w3, gs)
                return jax.lax.ragged_dot(h, w2, gs)
            pos = jnp.arange(x_sorted.shape[0])
            eid = jnp.searchsorted(jnp.cumsum(counts), pos, side='right')
            out = jnp.zeros((x_sorted.shape[0], w2.shape[-1]), x_sorted.dtype)
            for e in range(w1.shape[0]):
                xm = jnp.where((eid == e)[:, None], x_sorted, 0.0)
                he = jax.nn.silu(xm @ w1[e]) * (xm @ w3[e])
                out = out + he @ w2[e]
            return out
        x = hidden_states.reshape(-1, D)
        N = x.shape[0]
        scores = jax.nn.softmax(x @ gate_w.T, axis=-1)
        top_scores, sel = jax.lax.top_k(scores, K)
        sel_flat = sel.T.reshape(-1)
        scores_flat = top_scores.T.reshape(-1)
        order = jnp.argsort(sel_flat, stable=True)
        tok_sorted = order % N
        scores_sorted = scores_flat[order]
        counts = jnp.bincount(sel_flat, length=E)
        x_sorted = x[tok_sorted]
        y = _grouped_swiglu(x_sorted, counts, w1, w2, w3)
        weighted = y * scores_sorted[:, None]
        out = jnp.zeros((N, D), x.dtype).at[tok_sorted].add(weighted)
        return out.reshape(hidden_states.shape)
    h = _L0_tok_ref(x)
    h = jnp.concatenate([h, _L0_txt_ref(L0_txt_weight, x_txt)], axis=1)
    h = h + _L0_attn_ref(_layernorm(h, axis=-1), L0_attn_Wq, L0_attn_bq, L0_attn_Wk, L0_attn_bk, L0_attn_Wv, L0_attn_bv, L0_attn_Wo, L0_attn_bo, L0_attn_pos_bias)
    h = h + _L0_ffn_ref(_layernorm(h, axis=-1), L0_ffn_gate_w, L0_ffn_w1, L0_ffn_w2, L0_ffn_w3)
    return h

_drawn_inputs = setup_inputs


def setup_inputs(seed=0):
    import zlib

    import numpy as np

    out = dict(_drawn_inputs(seed))
    spreads = {'L0_attn_bq': (0.0, 0.8),
     'L0_attn_bk': (0.0, 2.0),
     'L0_attn_bv': (0.0, 0.1),
     'L0_attn_bo': (0.0, 0.1)}
    factors = {'L0_attn_Wq': 6.041, 'L0_attn_Wk': 5.615, 'L0_attn_pos_bias': 24.569}
    for name, (base, spread) in spreads.items():
        noise = np.random.default_rng([zlib.crc32(name.encode()), seed]).standard_normal(out[name].shape)
        drawn = base * np.exp(spread * noise) if base else spread * noise
        out[name] = jnp.asarray(drawn.astype(out[name].dtype))
    for name, factor in factors.items():
        out[name] = (out[name] * factor).astype(out[name].dtype)
    return out
```

```python
from contextlib import ExitStack

import concourse.bass as bass
from concourse import mybir

F32 = mybir.dt.float32
BF16 = mybir.dt.bfloat16
I32 = mybir.dt.int32
U32 = mybir.dt.uint32
ALU = mybir.AluOpType
ACT = mybir.ActivationFunctionType
AX = mybir.AxisListType

P = 128
B, IMG, D = 16, 256, 256
TXT = 77
S = IMG + TXT
H, HD = 16, 16
WIN, STRIDE = 128, 64
STARTS = [i * STRIDE for i in range((S - WIN) // STRIDE + 1)] + [S - WIN]
NW = len(STARTS)
GH = 4
NG = H // GH
G = NW * NG
C = D // P
TILES = [(0, P), (P, P), (2 * P, TXT)]
NT = len(TILES)
Q_SLOTS = (0, 1, 2, 0, 1, 0)
K_SLOTS = (0, 0, 0, 1, 1, 2)
KROWS = HD * len(Q_SLOTS)
VW = 48
VCOLS = H // 2 * VW
SCALE = float(HD) ** -0.5
EPS = 1e-5

E, K, HID = 8, 2, 512
HC = HID // P
TOKENS = B * S
REGION = TOKENS + P
ROW = D + 2
MT = TOKENS * K // P + E
BIG = 3.0e38


def group_heads(g):
    return [8 * (g // 2) + g % 2 + 2 * i for i in range(GH)]


def build(nc, x, x_txt, table, Wq, bq, Wk, bk, Wv, bv, Wo, bo, pos_bias, gate_wT, w1, w2, w3, use, out):
    ctx = ExitStack()
    with ctx:
        def sb(name, shape, dt=F32):
            return ctx.enter_context(nc.sbuf_tensor(name, shape, dt))

        def pb(name, shape):
            return ctx.enter_context(nc.psum_tensor(name, shape, F32))

        def sem(name):
            return ctx.enter_context(nc.semaphore(name))

        slots_dram = nc.dram_tensor("expert_slots", [E * REGION + P, ROW], F32, kind="Internal").ap()

        parts_dram = nc.dram_tensor("qk_parts", [2, D, 3, S], BF16, kind="Internal").ap()
        LOADS = 16 * 12
        STACK_IN = 16 * 2 * len(Q_SLOTS)

        stacks = sb("stacks", [P, 4 * H * S], BF16)
        q_stack = [stacks[:, (2 * i) * H * S:(2 * i + 1) * H * S].rearrange("p (h s) -> p h s", h=H) for i in range(2)]
        k_stack = [stacks[:, (2 * i + 1) * H * S:(2 * i + 2) * H * S].rearrange("p (h s) -> p h s", h=H) for i in range(2)]
        w2_sb = stacks[:, 0:2 * E * HC * D].bitcast(F32).rearrange("p (e c n) -> p e c n", e=E, c=HC)
        v_all = sb("v_all", [P, 2 * NW * VCOLS])
        v_win = [v_all[:, i * NW * VCOLS:(i + 1) * NW * VCOLS].rearrange("p (w n) -> p w n", w=NW) for i in range(2)]
        w1_sb = sb("w1_sb", [P, E, C, HID])
        w3_sb = sb("w3_sb", [P, E, C, HID])
        wq_sb = sb("wq_sb", [P, C, D])
        wk_sb = sb("wk_sb", [P, C, D])
        wv_sb = sb("wv_sb", [P, C, D])
        wo_sb = sb("wo_sb", [P, C, D])
        gate_sb = sb("gate_sb", [P, C, E])
        bq_col = sb("bq_col", [P, C])
        bk_col = sb("bk_col", [P, C])
        bv_row = sb("bv_row", [P, D])
        bo_row = sb("bo_row", [P, D])
        nbias = sb("nbias", [P, H, WIN])
        inv_use = sb("inv_use", [P, NW])
        ident = sb("ident", [P, P])
        before = sb("before", [P, P], BF16)
        ones = sb("ones", [P, P], BF16)
        expert_no = sb("expert_no", [P, E])
        lane = sb("lane", [P, 1])
        lane_i = sb("lane_i", [P, 1], I32)
        expert_i = sb("expert_i", [P, E], I32)
        token_i = sb("token_i", [P, NT], I32)
        text_ok = sb("text_ok", [P, 1])

        x_here = sb("x_here", [P, 2, IMG + 1])
        x_below = sb("x_below", [P, 2, IMG + 1])
        diag = sb("diag", [P, 2, IMG])
        anti = sb("anti", [P, 2, IMG])
        text_idx = sb("text_idx", [P, 1], I32)
        h_in = sb("h_in", [P, NT, D])
        h_res = [sb(f"h_res{i}", [P, NT, D]) for i in range(2)]
        stats1 = sb("stats1", [P, NT, 6])
        moments1 = sb("moments1", [P, NT, 2])
        rstd1 = sb("rstd1", [P, NT])
        var_eps = sb("var_eps", [P, NT])
        root_tmp = sb("root_tmp", [P, NT])
        xn = sb("xn", [P, NT, D])
        xT = sb("xT", [P, C, S])
        qk = sb("qk", [P, 2 * C, S])
        rest = sb("rest", [P, C, S])
        parts = sb("parts", [P, 2 * C, 3, S], BF16)

        probs = sb("probs", [P, 4, GH * WIN])
        neg_max = sb("neg_max", [P, 4, GH])
        row_sum = sb("row_sum", [P, 2, H])
        inv_sum = sb("inv_sum", [P, 2, H])
        weight = sb("weight", [P, 2, H, HD])
        probsT = sb("probsT", [P, 2, GH * WIN])
        weightT = sb("weightT", [P, C * WIN])
        head_out = sb("head_out", [P, 2, C * WIN])
        ctxT = sb("ctxT", [P, C, S])

        stats2 = sb("stats2", [P, NT, 6])
        moments2 = sb("moments2", [P, NT, 2])
        rstd2 = sb("rstd2", [P, NT])
        rows = sb("rows", [P, K, NT, ROW])
        x2T = rest
        gateT = xT[0:E, 0, :]
        logits = sb("logits", [P, NT, E])
        best = sb("best", [P, NT, E])
        best_i = sb("best_i", [P, NT, E], U32)
        pick = sb("pick", [P, NT, K])
        onehot = sb("onehot", [P, K, NT, E])
        taken = sb("taken", [P, NT, E], BF16)
        below_best = sb("below_best", [P, NT, E])
        score_e = sb("score_e", [P, NT, E])
        score_sum = sb("score_sum", [P, NT])
        score_inv = sb("score_inv", [P, NT])
        place = sb("place", [P, NT, E])
        place_k = sb("place_k", [P, K, NT, E])
        slot_f = sb("slot_f", [P, K, NT])
        slot_i = sb("slot_i", [P, K, NT], I32)
        token_f = sb("token_f", [P, NT])
        region_end = sb("region_end", [P, E])

        tile_no, tab_a, tab_b, tab_e = (qk[:, i, 0:MT] for i in range(4))
        row_tab, exp_tab = (qk[:, i, MT:2 * MT].bitcast(I32) for i in range(2))
        tile_i = sb("tile_i", [P, MT], I32)
        n_rows = sb("n_rows", [P, E])
        n_rows_i = sb("n_rows_i", [P, E], I32)
        n_tiles = sb("n_tiles", [P, E])
        tiles_to = sb("tiles_to", [P, E])
        tile_base = sb("tile_base", [P, E])
        pad_slot = sb("pad_slot", [P, E])
        pad_slot_i = sb("pad_slot_i", [P, E], I32)
        pad_rows = sb("pad_rows", [P, ROW])
        off = 0
        g_rows, gxT, hid, hidT, y_sb = [], [], [], [], []
        for lst, n in ((g_rows, ROW), (gxT, D), (hid, HID), (hidT, HID), (y_sb, D)):
            for i in range(2):
                lst.append(v_all[:, off:off + n])
                off += n
        assert off <= 2 * NW * VCOLS

        s_bank = pb("s_bank", [P, 2, 512])
        t_bank = pb("t_bank", [P, 2, 512])
        o_bank = pb("o_bank", [P, 2, 512])
        m_bank = pb("m_bank", [P, 2, 512])

        weights_in = sem("weights_in")
        bias_in = sem("bias_in")
        const_set = sem("const_set")
        const2_set = sem("const2_set")
        zeroed = sem("zeroed")
        psum_zeroed = sem("psum_zeroed")
        prep_done = sem("prep_done")
        x_in = sem("x_in")
        idx_in = sem("idx_in")
        text_in = sem("text_in")
        diffs_ready = sem("diffs_ready")
        conv_step = sem("conv_step")
        image_ready = sem("image_ready")
        ln1_step = sem("ln1_step")
        root1_step = sem("root1_step")
        rstd1_ready = sem("rstd1_ready")
        root2_step = sem("root2_step")
        rstd2_ready = sem("rstd2_ready")
        xn_ready = sem("xn_ready")
        res_ready = sem("res_ready")
        xT_done = sem("xT_done")
        xT_ready = sem("xT_ready")
        qk_done = sem("qk_done")
        qk_ready = sem("qk_ready")
        part1_ready = sem("part1_ready")
        rest_ready = sem("rest_ready")
        part2_ready = sem("part2_ready")
        part3_ready = sem("part3_ready")
        parts_out = sem("parts_out")
        stack_in = sem("stack_in")
        v_done = sem("v_done")
        v_ready = sem("v_ready")
        v_shift_in = sem("v_shift_in")
        scores_done = sem("scores_done")
        max_ready = sem("max_ready")
        exp_ready = sem("exp_ready")
        pT_done = sem("pT_done")
        pT_by_act = sem("pT_by_act")
        pT_by_dve = sem("pT_by_dve")
        pv_done = sem("pv_done")
        sum_step = sem("sum_step")
        weight_ready = sem("weight_ready")
        weightT_done = sem("weightT_done")
        weightT_ready = sem("weightT_ready")
        head_ready = sem("head_ready")
        ctx_zero = sem("ctx_zero")
        ctx_added = sem("ctx_added")
        wo_done = sem("wo_done")
        h2_ready = sem("h2_ready")
        h2_stored = sem("h2_stored")
        ln2_step = sem("ln2_step")
        rows0_ready = sem("rows0_ready")
        rows1_ready = sem("rows1_ready")
        x2T_done = sem("x2T_done")
        x2T_ready = sem("x2T_ready")
        gate_done = sem("gate_done")
        gate_ready = sem("gate_ready")
        logits_done = sem("logits_done")
        route_step = sem("route_step")
        taken_ready = sem("taken_ready")
        below_ready = sem("below_ready")
        score_e_ready = sem("score_e_ready")
        prefix_done = sem("prefix_done")
        place_step = sem("place_step")
        prefix_read = sem("prefix_read")
        token_step = sem("token_step")
        slots_ready = sem("slots_ready")
        payload_ready = sem("payload_ready")
        scattered = sem("scattered")

        pads_ready = sem("pads_ready")
        pads_in = sem("pads_in")
        table_step = sem("table_step")
        table_ready = sem("table_ready")
        w2_in = sem("w2_in")
        slot_in = [sem(f"slot_in{i}") for i in range(2)]
        gxT_done = sem("gxT_done")
        gxT_ready = sem("gxT_ready")
        up_done = sem("up_done")
        silu_ready = sem("silu_ready")
        hid_ready = sem("hid_ready")
        hidT_done = sem("hidT_done")
        hidT_ready = sem("hidT_ready")
        y_done = sem("y_done")
        y_ready = sem("y_ready")
        y_added = sem("y_added")

        passed = sem("passed")

        block = ctx.enter_context(nc.Block())

        PEEL_END = B + 1

        def wait_apart(eng, semaphore, value):
            eng.wait_ge(semaphore, value)
            if not isinstance(value, int):
                eng.sem_inc(passed, 1)

        def run_steps(eng, step):
            for b in (-2, -1, 0):
                step(b, b % 2)
            with eng.Fori(0, 6) as i:
                step(i * 2 + 1, 1)
                step(i * 2 + 2, 0)
            for b in range(13, PEEL_END):
                step(b, b % 2)

        def has(b):
            if not isinstance(b, int):
                return True, True, True, True
            return 0 <= b < B, 1 <= b <= B, 0 <= b + 1 < B, 0 <= b + 2 < B

        @block.sync
        def _(sp):
            for dst, src in ((wq_sb, Wq), (wk_sb, Wk), (wv_sb, Wv), (wo_sb, Wo)):
                sp.dma_start(dst[:, :, :], src.rearrange("(c p) n -> p c n", p=P)).then_inc(weights_in, 16)
            sp.dma_start(gate_sb[:, :, :], gate_wT.rearrange("(c p) n -> p c n", p=P)).then_inc(weights_in, 16)
            for dst, src in ((bq_col, bq), (bk_col, bk)):
                for c in range(C):
                    sp.dma_start(dst[:, c:c + 1], src[c * P:(c + 1) * P].rearrange("(p a) -> p a", a=1))\
                        .then_inc(weights_in, 16)
            sp.dma_start(bv_row[:, :], bv.partition_broadcast(P)).then_inc(weights_in, 16)
            sp.dma_start(bo_row[:, :], bo.partition_broadcast(P)).then_inc(weights_in, 16)
            sp.dma_start(inv_use[:, :], use).then_inc(weights_in, 16)
            sp.dma_start(nbias[:, :, :], pos_bias.rearrange("h q k -> q h k")).then_inc(bias_in, 16)
            sp.wait_ge(zeroed, 7)

            def step(b, par):
                att, tail, proj, inp = has(b)
                if inp:
                    b2 = b + 2
                    if not isinstance(b, int) or b2 >= 1:
                        wait_apart(sp, diffs_ready, b2 * 2)
                        wait_apart(sp, text_in, b2 * 16)
                    if isinstance(b, int):
                        img, txt = x[b2], x_txt[b2]
                    else:
                        img = x[bass.ds(b2, 1)].rearrange("a r c -> (a r) c")
                        txt = x_txt[bass.ds(b2, 1)].rearrange("a t -> (a t)")
                    sp.dma_start(x_here[:, :, 0:IMG], img.rearrange("(j p) c -> p j c", p=P)).then_inc(x_in, 16)
                    sp.dma_start(x_below[:, 0, 0:IMG], img[1:P + 1, :]).then_inc(x_in, 16)
                    sp.dma_start(x_below[0:112, 1, 0:IMG], img[P + 1:P + 113, :]).then_inc(x_in, 16)
                    sp.dma_start(x_below[112:127, 1, 0:IMG], img[P + 113:IMG, :]).then_inc(x_in, 16)
                    sp.dma_start(text_idx[0:TXT, :], txt.rearrange("(t a) -> t a", a=1)).then_inc(idx_in, 16)
                if proj:
                    b1, par1 = b + 1, 1 - par
                    for n, (dst, slots) in enumerate([(q_stack[par1], Q_SLOTS), (k_stack[par1], K_SLOTS)]):
                        wait_apart(sp, part3_ready, b1 * 2 + n + 1)
                        if n == 0 and (not isinstance(b, int) or b1 >= 1):
                            wait_apart(sp, stack_in, b1 * STACK_IN)
                        sp.dma_start(parts_dram[n].rearrange("(c p) t s -> p c t s", p=P),
                                     parts[:, 2 * n:2 * n + 2, :, :]).then_inc(parts_out, 16)
                        if n == 0 and (not isinstance(b, int) or b >= 1):
                            wait_apart(sp, scores_done, (b1 - 1) * G)
                        wait_apart(sp, parts_out, b1 * 32 + 16 * n + 16)
                        for s, part in enumerate(slots):
                            sp.dma_start(dst[s * HD:(s + 1) * HD, :, :],
                                         parts_dram[n, :, part, :].rearrange("(h d) s -> d h s", d=HD))\
                                .then_inc(stack_in, 16)
                        if n == 0:
                            vt = v_win[par1]
                            wait_apart(sp, v_ready, b1 * 3 + 3)
                            sp.dma_start(vt[0:64, 1, :], vt[64:128, 0, :]).then_inc(v_shift_in, 16)
                            sp.dma_start(vt[64:128, 1, :], vt[0:64, 2, :]).then_inc(v_shift_in, 16)
                            sp.dma_start(vt[0:64, 3, :], vt[64:128, 2, :]).then_inc(v_shift_in, 16)
                            o = STARTS[3] + 64 - STARTS[4]
                            sp.dma_start(vt[64:128, 3, :], vt[o:o + 64, 4, :]).then_inc(v_shift_in, 16)
                if tail:
                    b0, hr = b - 1, h_res[1 - par]
                    wait_apart(sp, h2_ready, b0 * 2 + 2)
                    if isinstance(b, int):
                        dst = out[b0 * S:(b0 + 1) * S, :]
                    else:
                        dst = out[bass.ds(b0 * S, S), :]
                    sp.dma_start(dst[0:IMG, :].rearrange("(j p) n -> p j n", p=P), hr[:, 0:2, :]).then_inc(h2_stored, 16)
                    sp.dma_start(dst[IMG:S, :], hr[0:TXT, 2, :]).then_inc(h2_stored, 16)

            run_steps(sp, step)

            sp.wait_ge(scores_done, B * G)
            for e in range(E):
                sp.dma_start(w2_sb[:, e], w2[e].rearrange("(c p) n -> p c n", p=P)).then_inc(w2_in, 16)
            sp.wait_ge(pads_in, 16 * (E + 2))
            sp.wait_ge(scattered, 96 * B)
            sp.wait_ge(table_ready, 1)

            def load_tile(t, par, reused):
                row = sp.value_load(row_tab[0:1, bass.ds(t, 1)], min_val=0, max_val=E * REGION)
                if reused:
                    wait_apart(sp, y_added, t * 16 - 16)
                sp.dma_start(g_rows[par], slots_dram[bass.ds(row, P), :]).then_inc(slot_in[par], 16)

            load_tile(0, 0, False)
            load_tile(1, 1, False)
            with sp.Fori(0, (MT - 3) // 2) as i:
                load_tile(i * 2 + 2, 0, True)
                load_tile(i * 2 + 3, 1, True)
            load_tile(MT - 1, 0, True)
            sp.wait_ge(h2_stored, 32 * B)

        @block.gpsimd
        def _(pool):
            pool.memset(ident[:, :], 0.0).then_inc(const_set, 1)
            pool.memset(before[:, :], 1.0).then_inc(const_set, 1)
            pool.memset(ones[:, :], 1.0).then_inc(const_set, 1)
            pool.memset(text_ok[:, :], 1.0).then_inc(const_set, 1)
            pool.iota(expert_i[:, :], pattern=[[1, E]], base=0, channel_multiplier=0).then_inc(const_set, 1)
            pool.iota(lane_i[:, :], pattern=[[0, 1]], base=0, channel_multiplier=1).then_inc(const_set, 1)
            pool.iota(token_i[:, :], pattern=[[P, NT]], base=0, channel_multiplier=1).then_inc(const_set, 1)
            pool.iota(tile_i[:, :], pattern=[[1, MT]], base=0, channel_multiplier=0).then_inc(const_set, 1)
            pool.wait_ge(const_set, 8)
            pool.affine_select(out=ident[:, :], in_=ident[:, :], compare_op=ALU.not_equal, fill=1.0,
                               base=0, pattern=[[-1, P]], channel_multiplier=1).then_inc(const_set, 1)
            pool.affine_select(out=before[:, :], in_=before[:, :], compare_op=ALU.is_gt, fill=0.0,
                               base=0, pattern=[[1, P]], channel_multiplier=-1).then_inc(const_set, 1)
            pool.affine_select(out=text_ok[:, :], in_=text_ok[:, :], compare_op=ALU.is_gt, fill=0.0,
                               base=TXT, pattern=[[0, 1]], channel_multiplier=-1).then_inc(const_set, 1)
            pool.memset(x_here[:, :, :], 0.0).then_inc(zeroed, 1)
            pool.memset(x_below[:, :, :], 0.0).then_inc(zeroed, 1)
            pool.memset(h_in[:, :, :], 0.0).then_inc(zeroed, 1)
            pool.memset(v_all[:, :], 0.0).then_inc(zeroed, 1)
            pool.memset(pad_rows[:, 0:D + 1], 0.0).then_inc(zeroed, 1)
            pool.memset(rows[:, :, :, D:ROW], 0.0).then_inc(zeroed, 1)
            pool.memset(text_idx[:, :], 0).then_inc(zeroed, 1)
            pool.wait_ge(zeroed, 7)
            pool.wait_ge(weights_in, LOADS)
            pool.wait_ge(const2_set, 5)
            pool.dma_start(slots_dram[E * REGION:E * REGION + P, :], pad_rows[:, :]).then_inc(pads_in, 16)
            pool.dma_start(out[TOKENS:TOKENS + P, :], pad_rows[:, 0:D]).then_inc(pads_in, 16)
            NEWTON = 3
            ROOT = 2 + 4 * NEWTON

            def inverse_root(moments, rstd, chain, b, done):
                first = b * (ROOT - 1)
                pool.tensor_scalar(var_eps[:, :], moments[:, :, 1], EPS, None, ALU.add).then_inc(chain, 1)
                wait_apart(pool, chain, first + 1)
                pool.tensor_scalar(rstd[:, :].bitcast(I32), var_eps[:, :].bitcast(I32), -0.5, float(0x5F3759DF),
                                   ALU.mult, ALU.add).then_inc(chain, 1)
                for i in range(NEWTON):
                    pool.wait_ge(chain, first + 2 + 4 * i)
                    pool.tensor_tensor(root_tmp[:, :], rstd[:, :], rstd[:, :], ALU.mult).then_inc(chain, 1)
                    pool.wait_ge(chain, first + 3 + 4 * i)
                    pool.tensor_tensor(root_tmp[:, :], root_tmp[:, :], var_eps[:, :], ALU.mult).then_inc(chain, 1)
                    wait_apart(pool, chain, first + 4 + 4 * i)
                    pool.tensor_scalar(root_tmp[:, :], root_tmp[:, :], -0.5, 1.5, ALU.mult, ALU.add).then_inc(chain, 1)
                    pool.wait_ge(chain, first + 5 + 4 * i)
                    ins = pool.tensor_tensor(rstd[:, :], rstd[:, :], root_tmp[:, :], ALU.mult)
                    ins.then_inc(chain if i < NEWTON - 1 else done, 1)

            def step(b, par):
                att, tail, proj, inp = has(b)
                known = isinstance(b, int)
                for k in range(G):
                    if inp and k == 2:
                        b2 = b + 2
                        pool.wait_ge(x_in, b2 * 64 + 64)
                        if not known or b2 >= 1:
                            pool.wait_ge(image_ready, b2)
                        pool.tensor_tensor(diag[:, :, :], x_here[:, :, 0:IMG], x_below[:, :, 1:IMG + 1],
                                           ALU.subtract).then_inc(diffs_ready, 1)
                        pool.tensor_tensor(anti[:, :, :], x_below[:, :, 0:IMG], x_here[:, :, 1:IMG + 1],
                                           ALU.subtract).then_inc(diffs_ready, 1)
                    if proj and k in (3, 6):
                        n, b1 = (0, b + 1) if k == 3 else (1, b + 1)
                        pool.wait_ge(part1_ready, b1 * 2 + n + 1)
                        if n == 1 or not known or b1 >= 1:
                            pool.wait_ge(part3_ready, b1 * 2 + n)
                        if n == 0 and (not known or b1 >= 3):
                            pool.wait_ge(gate_done, b1 - 2)
                        pool.tensor_tensor(rest[:, :, :], qk[:, 2 * n:2 * n + 2, :], parts[:, 2 * n:2 * n + 2, 0, :],
                                           ALU.subtract).then_inc(rest_ready, 1)
                        pool.wait_ge(part2_ready, b1 * 2 + n + 1)
                        pool.tensor_tensor(parts[:, 2 * n:2 * n + 2, 2, :], rest[:, :, :],
                                           parts[:, 2 * n:2 * n + 2, 1, :], ALU.subtract).then_inc(part3_ready, 1)
                    v = (k - 5) // NG
                    if (k - 5) % NG == 3 and ((att and v >= 0) or (tail and v < 0)):
                        wv = b * NW + v
                        w = v % NW
                        pool.wait_ge(head_ready, wv + 1)
                        pool.wait_ge(ctx_zero, b + 1 if v >= 0 else b)
                        if w > 0:
                            pool.wait_ge(ctx_added, wv)
                        view = ctxT[:, :, STARTS[w]:STARTS[w] + WIN]
                        pool.tensor_tensor(view, view, head_out[:, (par + v) % 2, :].rearrange("p (c q) -> p c q", c=C),
                                           ALU.add).then_inc(ctx_added, 1)
                    if att and k == 7:
                        if not known or b >= 1:
                            wait_apart(pool, wo_done, b * 2)
                        pool.memset(ctxT[:, :, :], 0.0).then_inc(ctx_zero, 1)
                    if proj and k == 12:
                        b1 = b + 1
                        pool.wait_ge(image_ready, b1 + 1)
                        pool.wait_ge(text_in, b1 * 16 + 16)
                        if not known or b1 >= 2:
                            pool.wait_ge(h2_stored, (b1 - 1) * 32)
                            pool.wait_ge(rows0_ready, (b1 - 1) * 3)
                        pool.tensor_tensor(h_res[1 - par][:, :, :], h_in[:, :, :],
                                           bo_row[:, :].unsqueeze(1).to_broadcast([P, NT, D]), ALU.add)\
                            .then_inc(res_ready, 1)
                    if inp and k == 12:
                        b2 = b + 2
                        pool.wait_ge(idx_in, b2 * 16 + 16)
                        if not known or b2 >= 1:
                            pool.wait_ge(res_ready, b2)
                            wait_apart(pool, xn_ready, b2 * 3)
                        pool.indirect_dma_start(h_in[0:TXT, 2, :], None, table,
                                                bass.IndirectOffsetOnAxis(text_idx[0:TXT, 0:1], 0)).then_inc(text_in, 16)
                    if inp and k == 16:
                        if not known or b + 2 >= 1:
                            pool.wait_ge(xn_ready, b * 3 + 6)
                        wait_apart(pool, ln1_step, b * 6 + 18)
                        inverse_root(moments1, rstd1, root1_step, b + 2, rstd1_ready)
                    if tail and k == 9:
                        if not known or b >= 2:
                            pool.wait_ge(rows0_ready, b * 3 - 3)
                        wait_apart(pool, ln2_step, b * 6)
                        inverse_root(moments2, rstd2, root2_step, b - 1, rstd2_ready)
                    if tail and k == 13:
                        b0 = b - 1
                        pool.wait_ge(rows0_ready, b0 * 3 + 3)
                        if not known or b0 >= 1:
                            wait_apart(pool, scattered, b0 * 96)
                        pool.tensor_copy(rows[:, 1, :, 0:D], rows[:, 0, :, 0:D]).then_inc(rows1_ready, 1)
                    if tail and k == 19:
                        b0 = b - 1
                        pool.wait_ge(slots_ready, b0 + 1)
                        pool.wait_ge(payload_ready, b0 * 4 + 4)
                        wait_apart(pool, rows1_ready, b0 + 1)
                        for kk in range(K):
                            for j, (_, n) in enumerate(TILES):
                                pool.indirect_dma_start(slots_dram[:, :],
                                                        bass.IndirectOffsetOnAxis(slot_i[0:n, kk, j:j + 1], 0),
                                                        rows[0:n, kk, j, :], None).then_inc(scattered, 16)

            run_steps(pool, step)
            pool.wait_ge(pads_ready, 1)
            pool.wait_ge(scattered, 96 * B)
            for e in range(E):
                pool.indirect_dma_start(slots_dram[:, :], bass.IndirectOffsetOnAxis(pad_slot_i[:, e:e + 1], 0),
                                        pad_rows[:, :], None).then_inc(pads_in, 16)
            pool.wait_ge(h2_stored, 32 * B)

            def add_tile(t, par, first):
                pool.wait_ge(y_ready, t + 1)
                if not first:
                    wait_apart(pool, y_added, t * 16)
                pool.indirect_dma_start(out[:, :],
                                        bass.IndirectOffsetOnAxis(g_rows[par][:, D + 1:D + 2].bitcast(I32), 0),
                                        y_sb[par], None, compute_op=ALU.add).then_inc(y_added, 16)

            add_tile(0, 0, True)
            with pool.Fori(0, (MT - 1) // 2) as i:
                add_tile(i * 2 + 1, 1, False)
                add_tile(i * 2 + 2, 0, False)
            pool.wait_ge(y_added, 16 * MT)
            pool.wait_ge(pads_in, 16 * (E + 2))

        @block.scalar
        def _(act):
            for e in range(E):
                act.dma_start(w1_sb[:, e], w1[e].rearrange("(c p) n -> p c n", p=P)).then_inc(w2_in, 16)
                act.dma_start(w3_sb[:, e], w3[e].rearrange("(c p) n -> p c n", p=P)).then_inc(w2_in, 16)
            act.wait_ge(prep_done, 2)

            def step(b, par):
                att, tail, proj, inp = has(b)
                known = isinstance(b, int)
                for k in range(G + 0):
                    if (k >= 1 and att) or (k < 1 and tail):
                        g = (k - 1) % NG
                        r = (k - 1) % 4
                        v = (k - 1) // NG
                        act.wait_ge(max_ready, b * G + k)
                        if g == 0 and (not known or b * NW + v >= 2):
                            act.wait_ge(sum_step, b * NW + v - 1)
                        for i, h in enumerate(group_heads(g)):
                            seg = probs[:, r, i * WIN:(i + 1) * WIN]
                            ins = act.activation(seg, seg, ACT.Exp, bias=neg_max[:, r, i:i + 1], scale=-1.0,
                                                 accum_out=row_sum[:, (par + v) % 2, h:h + 1])
                        ins.then_inc(exp_ready, 1)
                    g = (k - 2) % NG
                    if g != 3 and ((k >= 2 and att) or (k < 2 and tail)):
                        n = b * G + (k - 2)
                        act.wait_ge(pT_done, n + 1)
                        if not known or n >= 2:
                            act.wait_ge(pv_done, n - 1)
                        act.activation(probsT[:, k % 2, :], t_bank[:, k % 2, :], ACT.Copy).then_inc(pT_by_act, 1)
                    v = (k - 4) // NG
                    if (k - 4) % NG == 3 and ((att and v >= 0) or (tail and v < 0)):
                        act.wait_ge(weightT_done, b * NW + v + 1)
                        if not known or b * NW + v >= 1:
                            act.wait_ge(head_ready, b * NW + v)
                        act.activation(weightT[:, :], o_bank[:, (par + v) % 2, C * WIN:2 * C * WIN], ACT.Copy)\
                            .then_inc(weightT_ready, 1)
                    if proj and k == 0:
                        b1 = b + 1
                        act.wait_ge(xT_done, b1 + 1)
                        if not known or b1 >= 1:
                            act.wait_ge(v_done, b1 * 2)
                        if not known or b1 >= 3:
                            act.wait_ge(logits_done, b1 - 2)
                        act.activation(xT[:, :, :], m_bank[:, :, 0:S], ACT.Copy).then_inc(xT_ready, 1)
                    if proj and k in (2, 4):
                        b1, n = b + 1, k // 2 - 1
                        for c in range(C):
                            act.wait_ge(qk_done, b1 * 4 + 2 * n + c + 1)
                            if not known or b1 >= 1:
                                act.wait_ge(rest_ready, b1 * 2)
                            act.activation(qk[:, 2 * n + c, :], m_bank[:, c, 0:S], ACT.Identity,
                                           bias=(bq_col if n == 0 else bk_col)[:, c:c + 1],
                                           scale=(-SCALE if n == 0 else 1.0)).then_inc(qk_ready, 1)
                    if tail and k == 12:
                        act.wait_ge(x2T_done, b)
                        if proj:
                            act.wait_ge(part3_ready, b * 2 + 4)
                        act.activation(x2T[:, :, :], m_bank[:, :, 0:S], ACT.Copy).then_inc(x2T_ready, 1)
                    if tail and k == 14:
                        act.wait_ge(gate_done, b)
                        if proj:
                            act.wait_ge(v_done, b * 2 + 4)
                        act.activation(gateT, m_bank[0:E, 0, 0:S], ACT.Copy).then_inc(gate_ready, 1)
                    if tail and k == 17:
                        act.wait_ge(below_ready, b)
                        if not known or b >= 2:
                            act.wait_ge(payload_ready, (b - 1) * 4)
                        act.activation(score_e[:, :, :], below_best[:, :, :], ACT.Exp).then_inc(score_e_ready, 1)

            run_steps(act, step)

            def silu_tile(t, par):
                act.wait_ge(up_done, t + 1)
                if not isinstance(t, int) or t >= 2:
                    act.wait_ge(hidT_done, t - 1)
                act.activation(hid[par], s_bank[:, par, :], ACT.Silu).then_inc(silu_ready, 1)

            def gxT_tile(t, par):
                act.wait_ge(gxT_done, t + 1)
                if not isinstance(t, int) or t >= 2:
                    act.wait_ge(up_done, t - 1)
                act.activation(gxT[par], m_bank[:, 0, 0:D], ACT.Copy).then_inc(gxT_ready, 1)

            gxT_tile(0, 0)
            silu_tile(0, 0)
            gxT_tile(1, 1)
            with act.Fori(0, (MT - 3) // 2) as i:
                for u in range(2):
                    silu_tile(i * 2 + 1 + u, 1 - u)
                    gxT_tile(i * 2 + 2 + u, u)
            silu_tile(MT - 2, 1)
            gxT_tile(MT - 1, 0)
            silu_tile(MT - 1, 0)

        @block.vector
        def _(dve):
            for bank in (s_bank, t_bank, o_bank, m_bank):
                dve.memset(bank[:, :, :], 0.0).then_inc(psum_zeroed, 1)
            dve.wait_ge(const_set, 11)
            dve.tensor_copy(expert_no[:, :], expert_i[:, :]).then_inc(const2_set, 1)
            dve.tensor_copy(token_f[:, :], token_i[:, :]).then_inc(const2_set, 1)
            dve.tensor_scalar(pad_rows[:, D + 1:D + 2].bitcast(I32), lane_i[:, :], float(TOKENS), None, ALU.add)\
                .then_inc(const2_set, 1)
            dve.tensor_scalar(region_end[:, :], expert_i[:, :], float(REGION), None, ALU.mult).then_inc(const2_set, 1)
            dve.tensor_copy(lane[:, :], lane_i[:, :]).then_inc(const2_set, 1)
            dve.wait_ge(const2_set, 5)
            dve.wait_ge(weights_in, LOADS)
            dve.tensor_scalar(bq_col[:, :], bq_col[:, :], -SCALE, None, ALU.mult).then_inc(prep_done, 1)
            dve.wait_ge(bias_in, 16)
            dve.tensor_scalar(nbias[:, :, :], nbias[:, :, :], -1.0, None, ALU.mult).then_inc(prep_done, 1)
            dve.wait_ge(prep_done, 2)
            dve.wait_ge(zeroed, 7)

            def moments_of(src, stats, moments, b, chain):
                for j in range(NT):
                    dve.bn_stats(stats[:, j, :], src[:, j, :]).then_inc(chain, 1)
                for j in range(NT):
                    wait_apart(dve, chain, b * 6 + 1 + j)
                    dve.bn_aggr(moments[:, j, :], stats[:, j, :]).then_inc(chain, 1)

            def normalise(src, moments, rstd, dst, done):
                for j in range(NT):
                    dve.tensor_scalar(dst(j), src[:, j, :], moments[:, j, 0:1], rstd[:, j:j + 1],
                                      ALU.subtract, ALU.mult).then_inc(done, 1)

            RS = 8
            PS = 3

            def step(b, par):
                att, tail, proj, inp = has(b)
                known = isinstance(b, int)
                for k in range(G):
                    if att:
                        g, r = k % NG, k % 4
                        dve.wait_ge(scores_done, b * G + k + 1)
                        if not known or b * G + k >= 4:
                            wait_apart(dve, pT_done, b * G + k - 3)
                        for i, h in enumerate(group_heads(g)):
                            ins = dve.tensor_tensor_reduce(probs[:, r, i * WIN:(i + 1) * WIN],
                                                           s_bank[:, k % 2, i * WIN:(i + 1) * WIN], nbias[:, h, :],
                                                           1.0, BIG, ALU.add, ALU.min, neg_max[:, r, i:i + 1])
                        ins.then_inc(max_ready, 1)
                    v = (k - 2) // NG
                    if (k - 2) % NG == 3 and ((att and v >= 0) or (tail and v < 0)):
                        n = b * G + (k - 2)
                        wv, vp = b * NW + v, (par + v) % 2
                        dve.wait_ge(exp_ready, n + 1)
                        dve.reciprocal(inv_sum[:, vp, :], row_sum[:, vp, :]).then_inc(sum_step, 1)
                        dve.wait_ge(pT_done, n + 1)
                        if not known or n >= 2:
                            dve.wait_ge(pv_done, n - 1)
                        dve.tensor_copy(probsT[:, k % 2, :], t_bank[:, k % 2, :]).then_inc(pT_by_dve, 1)
                        dve.wait_ge(sum_step, wv + 1)
                        if not known or wv >= 2:
                            dve.wait_ge(weightT_done, wv - 1)
                        dve.tensor_scalar(weight[:, vp, :, :], inv_sum[:, vp, :].unsqueeze(2).to_broadcast([P, H, HD]),
                                          inv_use[:, v % NW:v % NW + 1], None, ALU.mult).then_inc(weight_ready, 1)
                    v = (k - 5) // NG
                    if (k - 5) % NG == 3 and ((att and v >= 0) or (tail and v < 0)):
                        wv, vp = b * NW + v, (par + v) % 2
                        dve.wait_ge(weightT_ready, wv + 1)
                        if not known or wv >= 2:
                            dve.wait_ge(ctx_added, wv - 1)
                        dve.tensor_tensor(head_out[:, vp, :], o_bank[:, vp, 0:C * WIN], weightT[:, :], ALU.mult)\
                            .then_inc(head_ready, 1)
                    if proj and k in (3, 5):
                        n, b1 = (k - 3) // 2, b + 1
                        dve.wait_ge(qk_ready, b1 * 4 + 2 * n + 2)
                        if not known or b1 >= 1:
                            dve.wait_ge(parts_out, b1 * 32)
                        dve.tensor_copy(parts[:, 2 * n:2 * n + 2, 0, :], qk[:, 2 * n:2 * n + 2, :])\
                            .then_inc(part1_ready, 1)
                    if proj and k in (5, 8):
                        n, b1 = (0, b + 1) if k == 5 else (1, b + 1)
                        dve.wait_ge(rest_ready, b1 * 2 + n + 1)
                        dve.tensor_copy(parts[:, 2 * n:2 * n + 2, 1, :], rest[:, :, :]).then_inc(part2_ready, 1)
                    if proj and k == 6:
                        b1, vt = b + 1, v_win[1 - par]
                        if not known or b1 >= 2:
                            dve.wait_ge(pv_done, (b1 - 1) * G)
                        for n, w in enumerate((0, 2, 4)):
                            dve.wait_ge(v_done, b1 * 2 + 1 + n // 2)
                            cols = vt[:, w, :].rearrange("p (t a e) -> p t a e", a=3, e=HD)[:, :, 0:3:2, :]
                            src = m_bank[:, n // 2, (n % 2) * D:(n % 2) * D + D]
                            dve.tensor_tensor(cols, src.rearrange("p (t a e) -> p t a e", a=2, e=HD),
                                              bv_row[:, :].rearrange("p (t a e) -> p t a e", a=2, e=HD),
                                              ALU.add).then_inc(v_ready, 1)
                    if tail and k == 7:
                        b0, hr = b - 1, h_res[1 - par]
                        dve.wait_ge(wo_done, b0 * 2 + 1)
                        dve.wait_ge(res_ready, b0 + 1)
                        dve.tensor_tensor(hr[:, 0:2, :], m_bank[:, 0, :].rearrange("p (j n) -> p j n", j=2),
                                          hr[:, 0:2, :], ALU.add).then_inc(h2_ready, 1)
                        dve.wait_ge(wo_done, b0 * 2 + 2)
                        dve.tensor_tensor(hr[0:TXT, 2, :], m_bank[0:TXT, 1, 0:D], hr[0:TXT, 2, :], ALU.add)\
                            .then_inc(h2_ready, 1)
                    if tail and k == 8:
                        b0, hr = b - 1, h_res[1 - par]
                        dve.wait_ge(h2_ready, b0 * 2 + 2)
                        if not known or b0 >= 1:
                            dve.wait_ge(rows0_ready, b0 * 3)
                            dve.wait_ge(rstd2_ready, b0)
                        moments_of(hr, stats2, moments2, b0, ln2_step)
                    if tail and k == 11:
                        b0, hr = b - 1, h_res[1 - par]
                        dve.wait_ge(rstd2_ready, b0 + 1)
                        if not known or b0 >= 1:
                            dve.wait_ge(scattered, b0 * 96)
                            dve.wait_ge(x2T_done, b0)
                        normalise(hr, moments2, rstd2, lambda j: rows[:, 0, j, 0:D], rows0_ready)
                    if tail and k == 16:
                        b0 = b - 1
                        dve.wait_ge(logits_done, b0 + 1)
                        dve.tensor_copy(logits[:, :, :], m_bank[:, 1, 0:NT * E].rearrange("p (j e) -> p j e", j=NT))\
                            .then_inc(route_step, 1)
                        wait_apart(dve, route_step, b0 * RS + 1)
                        for j in range(NT):
                            dve.max(best[:, j, :], logits[:, j, :]).then_inc(route_step, 1)
                        for j in range(NT):
                            wait_apart(dve, route_step, b0 * RS + 2 + j)
                            dve.max_index(best_i[:, j, :], best[:, j, :], logits[:, j, :]).then_inc(route_step, 1)
                        if not known or b0 >= 1:
                            dve.wait_ge(score_e_ready, b0)
                        dve.tensor_tensor(below_best[:, :, :], best[:, :, :],
                                          best[:, :, 0:1].to_broadcast([P, NT, E]), ALU.subtract)\
                            .then_inc(below_ready, 1)
                        dve.wait_ge(route_step, b0 * RS + 7)
                        dve.tensor_copy(pick[:, :, :], best_i[:, :, 0:K]).then_inc(route_step, 1)
                    if tail and k == 17:
                        b0 = b - 1
                        dve.wait_ge(route_step, b0 * RS + 8)
                        for kk in range(K):
                            dve.tensor_tensor(onehot[:, kk, :, :],
                                              expert_no[:, :].unsqueeze(1).to_broadcast([P, NT, E]),
                                              pick[:, :, kk:kk + 1].to_broadcast([P, NT, E]), ALU.is_equal)\
                                .then_inc(place_step, 1)
                        dve.wait_ge(place_step, b0 * PS + 2)
                        dve.tensor_scalar(onehot[:, :, 2, :], onehot[:, :, 2, :], text_ok[:, 0:1], None, ALU.mult)\
                            .then_inc(place_step, 1)
                        dve.wait_ge(place_step, b0 * PS + 3)
                        dve.tensor_tensor(taken[:, :, :], onehot[:, 0, :, :], onehot[:, 1, :, :], ALU.add)\
                            .then_inc(taken_ready, 1)
                    if tail and k == 19:
                        b0 = b - 1
                        dve.wait_ge(prefix_done, b0 + 1)
                        dve.tensor_tensor(place[:, :, :], m_bank[:, 0, 0:NT * E].rearrange("p (j e) -> p j e", j=NT),
                                          region_end[:, :].unsqueeze(1).to_broadcast([P, NT, E]), ALU.add)\
                            .then_inc(prefix_read, 1)
                        dve.wait_ge(prefix_read, b0 * 4 + 1)
                        dve.tensor_tensor(region_end[:, :], region_end[:, :], m_bank[:, 0, NT * E:(NT + 1) * E], ALU.add)\
                            .then_inc(prefix_read, 1)
                        dve.tensor_tensor(place_k[:, :, :, :], onehot[:, :, :, :],
                                          place[:, :, :].unsqueeze(1).to_broadcast([P, K, NT, E]), ALU.mult)\
                            .then_inc(prefix_read, 1)
                        dve.wait_ge(prefix_read, b0 * 4 + 3)
                        dve.tensor_reduce(slot_f[:, :, :], place_k[:, :, :, :], AX.X, ALU.add).then_inc(prefix_read, 1)
                        dve.wait_ge(prefix_read, b0 * 4 + 4)
                        dve.tensor_copy(slot_i[:, :, :], slot_f[:, :, :]).then_inc(slots_ready, 1)
                        dve.wait_ge(score_e_ready, b0 + 1)
                        dve.tensor_reduce(score_sum[:, :], score_e[:, :, :], AX.X, ALU.add).then_inc(payload_ready, 1)
                        dve.wait_ge(payload_ready, b0 * 4 + 1)
                        dve.reciprocal(score_inv[:, :], score_sum[:, :]).then_inc(payload_ready, 1)
                        dve.wait_ge(payload_ready, b0 * 4 + 2)
                        dve.tensor_tensor(rows[:, :, :, D].rearrange("p k j -> p j k"), score_e[:, :, 0:K],
                                          score_inv[:, :].unsqueeze(2).to_broadcast([P, NT, K]), ALU.mult)\
                            .then_inc(payload_ready, 1)
                        dve.tensor_copy(rows[:, :, :, D + 1].bitcast(I32),
                                        token_f[:, :].unsqueeze(1).to_broadcast([P, K, NT])).then_inc(payload_ready, 1)
                        dve.wait_ge(payload_ready, b0 * 4 + 4)
                        dve.tensor_scalar(token_f[:, :], token_f[:, :], float(S), None, ALU.add).then_inc(token_step, 1)
                    if inp and k == 12:
                        b2 = b + 2
                        for n, d in enumerate((diag, anti)):
                            bits = d[:, :, :].bitcast(I32)
                            dve.wait_ge(diffs_ready, b2 * 2 + n + 1)
                            dve.tensor_scalar(bits, bits, 0x7FFFFFFF, None, ALU.bitwise_and).then_inc(conv_step, 1)
                    if inp and k == 13:
                        b2 = b + 2
                        dve.wait_ge(conv_step, b2 * 3 + 2)
                        dve.tensor_tensor(diag[:, :, :], diag[:, :, :], anti[:, :, :], ALU.add).then_inc(conv_step, 1)
                    if inp and k == 14:
                        b2 = b + 2
                        dve.wait_ge(conv_step, b2 * 3 + 3)
                        if not known or b2 >= 1:
                            dve.wait_ge(res_ready, b2)
                            dve.wait_ge(xn_ready, b2 * 3)
                        dve.tensor_scalar(h_in[:, 0:2, :], diag[:, :, :], 1.0, 0.0, ALU.min, ALU.max)\
                            .then_inc(image_ready, 1)
                    if inp and k == 15:
                        b2 = b + 2
                        dve.wait_ge(image_ready, b2 + 1)
                        dve.wait_ge(text_in, b2 * 16 + 16)
                        if not known or b2 >= 1:
                            dve.wait_ge(rstd1_ready, b2)
                        moments_of(h_in, stats1, moments1, b2, ln1_step)
                    if inp and k == 18:
                        b2 = b + 2
                        dve.wait_ge(rstd1_ready, b2 + 1)
                        if not known or b2 >= 1:
                            dve.wait_ge(xT_done, b2)
                        normalise(h_in, moments1, rstd1, lambda j: xn[:, j, :], xn_ready)

            run_steps(dve, step)

            steps = [0]

            def link(ins):
                steps[0] += 1
                ins.then_inc(table_step, 1)
                dve.wait_ge(table_step, steps[0])

            dve.wait_ge(prefix_read, B * 4)
            link(dve.tensor_scalar(pad_slot[:, :], region_end[:, :], lane[:, 0:1], None, ALU.add))
            dve.tensor_copy(pad_slot_i[:, :], pad_slot[:, :]).then_inc(pads_ready, 1)
            dve.wait_ge(rest_ready, 2 * B)
            link(dve.tensor_copy(tile_no, tile_i[:, :]))
            link(dve.tensor_scalar(tile_base[:, :], expert_no[:, :], float(REGION), None, ALU.mult))
            link(dve.tensor_tensor(n_rows[:, :], region_end[:, :], tile_base[:, :], ALU.subtract))
            link(dve.tensor_scalar(n_rows[:, :], n_rows[:, :], float(P - 1), None, ALU.add))
            link(dve.tensor_copy(n_rows_i[:, :], n_rows[:, :]))
            link(dve.tensor_scalar(n_rows_i[:, :], n_rows_i[:, :], P.bit_length() - 1, None, ALU.logical_shift_right))
            link(dve.tensor_copy(n_tiles[:, :], n_rows_i[:, :]))
            link(dve.tensor_copy(tiles_to[:, 0:1], n_tiles[:, 0:1]))
            for e in range(1, E):
                link(dve.tensor_tensor(tiles_to[:, e:e + 1], tiles_to[:, e - 1:e], n_tiles[:, e:e + 1], ALU.add))
            link(dve.tensor_scalar(tab_e, tile_no, tiles_to[:, 0:1], None, ALU.is_ge))
            link(dve.tensor_scalar(tab_b, tab_e, n_tiles[:, 0:1], None, ALU.mult))
            for e in range(1, E):
                link(dve.tensor_scalar(tab_a, tile_no, tiles_to[:, e:e + 1], None, ALU.is_ge))
                link(dve.tensor_tensor(tab_e, tab_e, tab_a, ALU.add))
                link(dve.scalar_tensor_tensor(out=tab_b, in0=tab_a, scalar=n_tiles[:, e:e + 1],
                                              in1=tab_b, op0=ALU.mult, op1=ALU.add))
            link(dve.tensor_tensor(tab_b, tile_no, tab_b, ALU.subtract))
            link(dve.tensor_scalar(tab_b, tab_b, float(P), None, ALU.mult))
            link(dve.scalar_tensor_tensor(out=tab_b, in0=tab_e, scalar=float(REGION), in1=tab_b,
                                          op0=ALU.mult, op1=ALU.add))
            link(dve.tensor_scalar(tab_b, tab_b, float(E * REGION), None, ALU.min))
            link(dve.tensor_copy(row_tab, tab_b))
            link(dve.tensor_scalar(tab_e, tab_e, float(E - 1), None, ALU.min))
            link(dve.tensor_copy(exp_tab, tab_e))
            dve.tensor_copy(tab_a, tab_e).then_inc(table_ready, 1)

            def hid_tile(t, par):
                dve.wait_ge(silu_ready, t + 1)
                dve.tensor_tensor(hid[par], hid[par], t_bank[:, par, :], ALU.mult).then_inc(hid_ready, 1)

            def hidT_tile(t, par):
                dve.wait_ge(hidT_done, t + 1)
                if not isinstance(t, int) or t >= 2:
                    dve.wait_ge(y_done, t - 1)
                dve.tensor_copy(hidT[par], o_bank[:, 0, :]).then_inc(hidT_ready, 1)

            def y_tile(t, par):
                dve.wait_ge(y_done, t + 1)
                if not isinstance(t, int) or t >= 2:
                    dve.wait_ge(y_added, t * 16 - 16)
                dve.wait_ge(slot_in[par], (t - par) * 8 + 16)
                dve.tensor_scalar(y_sb[par], o_bank[:, 1, 0:D], g_rows[par][:, D:D + 1], None, ALU.mult)\
                    .then_inc(y_ready, 1)

            hid_tile(0, 0)
            hidT_tile(0, 0)
            for t in (1, 2):
                hid_tile(t, t % 2)
                y_tile(t - 1, 1 - t % 2)
                hidT_tile(t, t % 2)
            with dve.Fori(1, (MT - 1) // 2) as i:
                for u in range(2):
                    t = i * 2 + u
                    hid_tile(t + 1, 1 - u)
                    y_tile(t, u)
                    hidT_tile(t + 1, 1 - u)
            y_tile(MT - 1, 0)

        @block.tensor
        def _(pe):
            pe.wait_ge(psum_zeroed, 4)
            pe.wait_ge(const_set, 11)
            pe.wait_ge(weights_in, LOADS)

            def step(b, par):
                att, tail, proj, inp = has(b)
                known = isinstance(b, int)
                for k in range(G):
                    if att:
                        n, g, w = b * G + k, k % NG, k // NG
                        if k == 0:
                            pe.wait_ge(stack_in, b * STACK_IN + STACK_IN)
                        if not known or n >= 2:
                            pe.wait_ge(max_ready, n - 1)
                        lo = STARTS[w]
                        for i, h in enumerate(group_heads(g)):
                            mm = pe.matmul(s_bank[:, k % 2, i * WIN:(i + 1) * WIN],
                                           q_stack[par][0:KROWS, h, lo:lo + WIN], k_stack[par][0:KROWS, h, lo:lo + WIN],
                                           start=True, stop=True)
                        mm.then_inc(scores_done, 1)
                    if (k >= 2 and att) or (k < 2 and tail):
                        n, r = b * G + (k - 2), (k - 2) % 4
                        pe.wait_ge(exp_ready, n + 1)
                        if not known or n >= 2:
                            if (k - 4) % NG == 3:
                                pe.wait_ge(pT_by_dve, b * NW + (k - 4) // NG + 1)
                            else:
                                pe.wait_ge(pT_by_act, (b * NW + (k - 4) // NG) * 3 + (k - 4) % NG + 1)
                        for i in range(GH):
                            mm = pe.transpose(t_bank[:, k % 2, i * WIN:(i + 1) * WIN],
                                              probs[:, r, i * WIN:(i + 1) * WIN], ident[:, :])
                        mm.then_inc(pT_done, 1)
                    if (k >= 3 and att) or (k < 3 and tail):
                        m, n = k - 3, b * G + (k - 3)
                        w, g = (m // NG) % NW, m % NG
                        vp, bp = (par + m // NG) % 2, par if m >= 0 else 1 - par
                        if g == 3:
                            pe.wait_ge(pT_by_dve, b * NW + m // NG + 1)
                        else:
                            pe.wait_ge(pT_by_act, (b * NW + m // NG) * 3 + g + 1)
                        if m == 0:
                            pe.wait_ge(v_ready, b * 3 + 3)
                            pe.wait_ge(v_shift_in, b * 64 + 64)
                        if g == 0 and (not known or b * NW + m // NG >= 2):
                            pe.wait_ge(head_ready, b * NW + m // NG - 1)
                        for i, h in enumerate(group_heads(g)):
                            c0 = (h // 2) * VW + (h % 2) * HD
                            mm = pe.matmul(o_bank[32 * i:32 * i + 32, vp, (g // 2) * WIN:(g // 2 + 1) * WIN],
                                           v_win[bp][:, w, c0:c0 + 2 * HD],
                                           probsT[:, (k - 1) % 2, i * WIN:(i + 1) * WIN],
                                           start=(g % 2 == 0), stop=(g % 2 == 1), skip_group_check=True)
                        mm.then_inc(pv_done, 1)
                        if g == 3:
                            pe.wait_ge(weight_ready, b * NW + m // NG + 1)
                            for c in range(C):
                                mm = pe.transpose(o_bank[:, vp, (C + c) * WIN:(C + c + 1) * WIN],
                                                  weight[:, vp, 8 * c:8 * c + 8, :].rearrange("p h d -> p (h d)"),
                                                  ident[:, :])
                            mm.then_inc(weightT_done, 1)
                    b1 = b + 1
                    if proj and k == 0:
                        pe.wait_ge(xn_ready, b1 * 3 + 3)
                        if not known or b1 >= 3:
                            pe.wait_ge(prefix_read, (b1 - 2) * 4)
                            pe.wait_ge(route_step, (b1 - 2) * 8)
                        for c in range(C):
                            for j, (t0, n) in enumerate(TILES):
                                mm = pe.transpose(m_bank[:, c, t0:t0 + n], xn[0:n, j, c * P:(c + 1) * P], ident[0:n, 0:n])
                        mm.then_inc(xT_done, 1)
                    if proj and k in (1, 3):
                        n = (k - 1) // 2
                        wt = wq_sb if n == 0 else wk_sb
                        for c in range(C):
                            if n == 0:
                                pe.wait_ge(xT_ready, b1 + 1)
                            else:
                                pe.wait_ge(qk_ready, b1 * 4 + c + 1)
                            for a in range(C):
                                mm = pe.matmul(m_bank[:, c, 0:S], wt[:, a, c * P:(c + 1) * P], xT[:, a, :],
                                               start=(a == 0), stop=(a == C - 1))
                            mm.then_inc(qk_done, 1)
                    if proj and k == 5:
                        for bank, o, w in ((0, 0, 0), (0, D, 2), (1, 0, 4)):
                            pe.wait_ge(qk_ready, b1 * 4 + 3 + bank)
                            for a in range(C):
                                mm = pe.matmul(m_bank[:, bank, o:o + D], xT[:, a, STARTS[w]:STARTS[w] + WIN],
                                               wv_sb[:, a, :], start=(a == 0), stop=(a == C - 1))
                            if w:
                                mm.then_inc(v_done, 1)
                    b0 = b - 1
                    if tail and k == 7:
                        pe.wait_ge(ctx_added, b0 * NW + NW)
                        if proj:
                            pe.wait_ge(v_ready, b1 * 3 + 3)
                        elif b0 >= 1:
                            pe.wait_ge(prefix_read, b0 * 4)
                            pe.wait_ge(route_step, b0 * 8)
                        for j, (t0, n) in enumerate(TILES):
                            for a in range(C):
                                mm = pe.matmul(m_bank[0:n, j // 2, (j % 2) * D:(j % 2) * D + D], ctxT[:, a, t0:t0 + n],
                                               wo_sb[:, a, :], start=(a == 0), stop=(a == C - 1))
                            if j:
                                mm.then_inc(wo_done, 1)
                    if tail and k == 11:
                        pe.wait_ge(rows0_ready, b0 * 3 + 3)
                        pe.wait_ge(h2_ready, b0 * 2 + 2)
                        for c in range(C):
                            for j, (t0, n) in enumerate(TILES):
                                mm = pe.transpose(m_bank[:, c, t0:t0 + n], rows[0:n, 0, j, c * P:(c + 1) * P],
                                                  ident[0:n, 0:n])
                        mm.then_inc(x2T_done, 1)
                    if tail and k == 13:
                        pe.wait_ge(x2T_ready, b0 + 1)
                        for a in range(C):
                            mm = pe.matmul(m_bank[0:E, 0, 0:S], gate_sb[:, a, :], x2T[:, a, :],
                                           start=(a == 0), stop=(a == C - 1))
                        mm.then_inc(gate_done, 1)
                    if tail and k == 15:
                        wait_apart(pe, gate_ready, b0 + 1)
                        for j, (t0, n) in enumerate(TILES):
                            mm = pe.transpose(m_bank[0:n, 1, j * E:(j + 1) * E], gateT[:, t0:t0 + n], ident[0:E, 0:E])
                        mm.then_inc(logits_done, 1)
                    if tail and k == 18:
                        pe.wait_ge(taken_ready, b0 + 1)
                        pe.matmul(m_bank[:, 0, 0:NT * E], before[:, :], taken[:, :, :].rearrange("p j e -> p (j e)"),
                                  start=True, stop=False, skip_group_check=True)
                        for j in range(NT):
                            mm = pe.matmul(m_bank[:, 0, (j + 1) * E:(NT + 1) * E].rearrange("p (r e) -> p r e", e=E),
                                           ones[:, :], taken[:, j:j + 1, :].to_broadcast([P, NT - j, E]),
                                           start=False, stop=(j == NT - 1), skip_group_check=True)
                        mm.then_inc(prefix_done, 1)

            run_steps(pe, step)

            pe.wait_ge(w2_in, 16 * 3 * E)
            pe.wait_ge(table_ready, 1)

            def gx_tile(t, par, i):
                pe.wait_ge(slot_in[par], (t - par) * 8 + 16)
                if not isinstance(t, int) or t >= 1:
                    pe.wait_ge(gxT_ready, t)
                for c in range(C):
                    mm = pe.transpose(m_bank[:, 0, c * P:(c + 1) * P], g_rows[par][:, c * P:(c + 1) * P], ident[:, :])
                mm.then_inc(gxT_done, 1)

            def up_tile(t, par):
                e = pe.value_load(exp_tab[0:1, bass.ds(t, 1)], min_val=0, max_val=E - 1)
                pe.wait_ge(gxT_ready, t + 1)
                if not isinstance(t, int) or t >= 2:
                    pe.wait_ge(hid_ready, t - 1)
                for bank, wt in ((s_bank, w1_sb), (t_bank, w3_sb)):
                    for a in range(C):
                        mm = pe.matmul(bank[:, par, :], gxT[par][:, a * P:(a + 1) * P],
                                       wt[:, bass.ds(e, 1), a, :].rearrange("p o n -> p (o n)"),
                                       start=(a == 0), stop=(a == C - 1))
                mm.then_inc(up_done, 1)

            def down_tile(t, par):
                e = pe.value_load(exp_tab[0:1, bass.ds(t, 1)], min_val=0, max_val=E - 1)
                pe.wait_ge(hid_ready, t + 1)
                if not isinstance(t, int) or t >= 1:
                    pe.wait_ge(hidT_ready, t)
                for a in range(HC):
                    mm = pe.transpose(o_bank[:, 0, a * P:(a + 1) * P], hid[par][:, a * P:(a + 1) * P], ident[:, :])
                mm.then_inc(hidT_done, 1)
                return e

            def out_tile(t, par, e):
                pe.wait_ge(hidT_ready, t + 1)
                if not isinstance(t, int) or t >= 1:
                    pe.wait_ge(y_ready, t)
                for a in range(HC):
                    mm = pe.matmul(o_bank[:, 1, 0:D], hidT[par][:, a * P:(a + 1) * P],
                                   w2_sb[:, bass.ds(e, 1), a, :].rearrange("p o n -> p (o n)"),
                                   start=(a == 0), stop=(a == HC - 1))
                mm.then_inc(y_done, 1)

            gx_tile(0, 0, 0)
            up_tile(0, 0)
            with pe.Fori(0, (MT - 1) // 2) as i:
                for u in range(2):
                    t = i * 2 + u
                    gx_tile(t + 1, 1 - u, 0)
                    e = down_tile(t, u)
                    up_tile(t + 1, 1 - u)
                    out_tile(t, u, e)
            e = down_tile(MT - 1, 0)
            out_tile(MT - 1, 0, e)


_INS = ["x", "x_txt", "L0_txt_weight", "L0_attn_Wq", "L0_attn_bq", "L0_attn_Wk", "L0_attn_bk", "L0_attn_Wv",
        "L0_attn_bv", "L0_attn_Wo", "L0_attn_bo", "L0_attn_pos_bias", "L0_ffn_gate_w", "L0_ffn_w1", "L0_ffn_w2",
        "L0_ffn_w3"]


def kernel(**inputs):
    import numpy as _np
    import concourse.bacc as _bacc
    from concourse import mybir as _mybir
    from concourse.bass_utils import run_bass_kernel_spmd as _run

    nc = _bacc.Bacc("TRN2", target_bir_lowering=False, num_devices=1)
    arrays, args = {}, []
    for name in _INS:
        a = _np.asarray(inputs[name])
        if name == "x":
            a = a.reshape(B, IMG, D)
        if name == "L0_ffn_gate_w":
            a = a.T
        a = _np.ascontiguousarray(a)
        arrays[f"in_{name}_dram"] = a
        args.append(nc.dram_tensor(f"in_{name}_dram", a.shape, _mybir.dt.from_np(a.dtype), kind="ExternalInput").ap())
    counts = _np.zeros((P, NW), _np.float32)
    for w, lo in enumerate(STARTS):
        for q in range(WIN):
            counts[q, w] = 1.0 / sum(s <= lo + q < s + WIN for s in STARTS)
    arrays["counts_dram"] = counts
    args.append(nc.dram_tensor("counts_dram", counts.shape, _mybir.dt.from_np(counts.dtype), kind="ExternalInput").ap())
    args.append(nc.dram_tensor("out_dram", (TOKENS + P, D), _mybir.dt.float32, kind="ExternalOutput").ap())
    build(nc, *args)
    r = _run(nc, [arrays], core_ids=[0])
    return r.results[0]["out_dram"][:TOKENS].reshape(B, S, D)
```

```python
from contextlib import ExitStack

import concourse.bass as bass
from concourse import mybir

F32 = mybir.dt.float32
BF16 = mybir.dt.bfloat16
I32 = mybir.dt.int32
U32 = mybir.dt.uint32
ALU = mybir.AluOpType
ACT = mybir.ActivationFunctionType
AX = mybir.AxisListType

P = 128
B, IMG, D = 16, 256, 256
TXT = 77
S = IMG + TXT
H, HD = 16, 16
WIN, STRIDE = 128, 64
STARTS = [i * STRIDE for i in range((S - WIN) // STRIDE + 1)] + [S - WIN]
NW = len(STARTS)
GH = 4
NG = H // GH
G = NW * NG
C = D // P
TILES = [(0, P), (P, P), (2 * P, TXT)]
NT = len(TILES)
Q_SLOTS = (0, 1, 2, 0, 1, 0)
K_SLOTS = (0, 0, 0, 1, 1, 2)
KROWS = HD * len(Q_SLOTS)
VW = 48
VCOLS = H // 2 * VW
SCALE = float(HD) ** -0.5
EPS = 1e-5

E, K, HID = 8, 2, 512
HC = HID // P
TOKENS = B * S
REGION = TOKENS + P
ROW = D + 2
MT = TOKENS * K // P + E
RING = 4
BIG = 3.0e38


def group_heads(g):
    return [8 * (g // 2) + g % 2 + 2 * i for i in range(GH)]


def build(nc, x, x_txt, table, Wq, bq, Wk, bk, Wv, bv, Wo, bo, pos_bias, gate_wT, w1, w2, w3, use, out):
    ctx = ExitStack()
    with ctx:
        def sb(name, shape, dt=F32):
            return ctx.enter_context(nc.sbuf_tensor(name, shape, dt))

        def pb(name, shape):
            return ctx.enter_context(nc.psum_tensor(name, shape, F32))

        def sem(name):
            return ctx.enter_context(nc.semaphore(name))

        slots_dram = nc.dram_tensor("expert_slots", [E * REGION + P, ROW], F32, kind="Internal").ap()

        parts_dram = nc.dram_tensor("qk_parts", [2, D, 3, S], BF16, kind="Internal").ap()
        LOADS = 16 * 12
        STACK_IN = 16 * 2 * len(Q_SLOTS)

        stacks = sb("stacks", [P, 4 * H * S], BF16)
        q_stack = [stacks[:, (2 * i) * H * S:(2 * i + 1) * H * S].rearrange("p (h s) -> p h s", h=H) for i in range(2)]
        k_stack = [stacks[:, (2 * i + 1) * H * S:(2 * i + 2) * H * S].rearrange("p (h s) -> p h s", h=H) for i in range(2)]
        w2_sb = stacks[:, 0:2 * E * HC * D].bitcast(F32).rearrange("p (e c n) -> p e c n", e=E, c=HC)
        v_all = sb("v_all", [P, 2 * NW * VCOLS])
        v_win = [v_all[:, i * NW * VCOLS:(i + 1) * NW * VCOLS].rearrange("p (w n) -> p w n", w=NW) for i in range(2)]
        w1_sb = sb("w1_sb", [P, E, C, HID])
        w3_sb = sb("w3_sb", [P, E, C, HID])
        wq_sb = sb("wq_sb", [P, C, D])
        wk_sb = sb("wk_sb", [P, C, D])
        wv_sb = sb("wv_sb", [P, C, D])
        wo_sb = sb("wo_sb", [P, C, D])
        gate_sb = sb("gate_sb", [P, C, E])
        bq_col = sb("bq_col", [P, C])
        bk_col = sb("bk_col", [P, C])
        bv_row = sb("bv_row", [P, D])
        bo_row = sb("bo_row", [P, D])
        nbias_flat = sb("nbias", [P, H * WIN])
        nbias = nbias_flat[:, :].rearrange("p (h k) -> p h k", h=H)
        inv_use = sb("inv_use", [P, NW])
        ident = sb("ident", [P, P])
        before = sb("before", [P, P], BF16)
        ones = sb("ones", [P, P], BF16)
        expert_no = sb("expert_no", [P, E])
        lane = sb("lane", [P, 1])
        lane_i = sb("lane_i", [P, 1], I32)
        expert_i = sb("expert_i", [P, E], I32)
        token_i = sb("token_i", [P, NT], I32)
        text_ok = sb("text_ok", [P, 1])

        x_here = sb("x_here", [P, 2, IMG + 1])
        x_below = sb("x_below", [P, 2, IMG + 1])
        diag = sb("diag", [P, 2, IMG])
        anti = sb("anti", [P, 2, IMG])
        text_idx = sb("text_idx", [P, 1], I32)
        h_in = sb("h_in", [P, NT, D])
        h_res = [sb(f"h_res{i}", [P, NT, D]) for i in range(2)]
        stats1 = sb("stats1", [P, NT, 6])
        moments1 = sb("moments1", [P, NT, 2])
        rstd1 = sb("rstd1", [P, NT])
        var_eps = sb("var_eps", [P, NT])
        root_tmp = sb("root_tmp", [P, NT])
        xn = sb("xn", [P, NT, D])
        xT = sb("xT", [P, C, S])
        qk = sb("qk", [P, 2 * C, S])
        rest = sb("rest", [P, C, S])
        parts = sb("parts", [P, 2 * C, 3, S], BF16)

        probs = sb("probs", [P, 4, GH * WIN])
        neg_max = sb("neg_max", [P, 4, GH])
        row_sum = sb("row_sum", [P, 2, H])
        inv_sum = sb("inv_sum", [P, 2, H])
        weight = sb("weight", [P, 2, H, HD])
        probsT = sb("probsT", [P, 2, GH * WIN])
        weightT = sb("weightT", [P, C * WIN])
        head_out = sb("head_out", [P, 2, C * WIN])
        ctxT = sb("ctxT", [P, C, S])

        stats2 = sb("stats2", [P, NT, 6])
        moments2 = sb("moments2", [P, NT, 2])
        rstd2 = sb("rstd2", [P, NT])
        rows = sb("rows", [P, K, NT, ROW])
        x2T = rest
        gateT = xT[0:E, 0, :]
        logits = sb("logits", [P, NT, E])
        best = sb("best", [P, NT, E])
        best_i = sb("best_i", [P, NT, E], U32)
        pick = sb("pick", [P, NT, K])
        onehot = sb("onehot", [P, K, NT, E])
        taken = sb("taken", [P, NT, E], BF16)
        below_best = sb("below_best", [P, NT, E])
        score_e = sb("score_e", [P, NT, E])
        score_sum = sb("score_sum", [P, NT])
        score_inv = sb("score_inv", [P, NT])
        place = sb("place", [P, NT, E])
        place_k = sb("place_k", [P, K, NT, E])
        slot_f = sb("slot_f", [P, K, NT])
        slot_i = sb("slot_i", [P, K, NT], I32)
        token_f = sb("token_f", [P, NT])
        region_end = sb("region_end", [P, E])

        tile_no, tab_b, tab_e = (qk[:, i, 0:MT] for i in (0, 2, 3))
        tab_ge = xn[:, :, :].rearrange("p j n -> p (j n)")[:, 0:MT * E].rearrange("p (t e) -> p t e", e=E)
        row_tab, exp_tab = (qk[:, i, MT:2 * MT].bitcast(I32) for i in range(2))
        tile_i = sb("tile_i", [P, MT], I32)
        n_rows = sb("n_rows", [P, E])
        n_rows_i = sb("n_rows_i", [P, E], I32)
        n_tiles = sb("n_tiles", [P, E])
        tiles_to = sb("tiles_to", [P, E])
        tile_base = sb("tile_base", [P, E])
        region_end_i = sb("region_end_i", [P, E], I32)
        pad_rows = sb("pad_rows", [P, ROW])
        g_rows = [nbias_flat[:, i * ROW:(i + 1) * ROW] for i in range(RING)]
        y_sb = [probs[:, i, 0:D] for i in range(RING)]
        off = 0
        gxT, hid, hidT = [], [], []
        for lst, n in ((gxT, D), (hid, HID), (hidT, HID)):
            for i in range(2):
                lst.append(v_all[:, off:off + n])
                off += n
        assert off <= 2 * NW * VCOLS

        s_bank = pb("s_bank", [P, 2, 512])
        t_bank = pb("t_bank", [P, 2, 512])
        o_bank = pb("o_bank", [P, 2, 512])
        m_bank = pb("m_bank", [P, 2, 512])

        weights_in = sem("weights_in")
        bias_in = sem("bias_in")
        const_set = sem("const_set")
        const2_set = sem("const2_set")
        zeroed = sem("zeroed")
        x_zeroed = sem("x_zeroed")
        psum_zeroed = sem("psum_zeroed")
        prep_done = sem("prep_done")
        x_in = sem("x_in")
        idx_in = sem("idx_in")
        text_in = sem("text_in")
        diffs_ready = sem("diffs_ready")
        conv_step = sem("conv_step")
        image_ready = sem("image_ready")
        ln1_step = sem("ln1_step")
        root1_step = sem("root1_step")
        rstd1_ready = sem("rstd1_ready")
        root2_step = sem("root2_step")
        rstd2_ready = sem("rstd2_ready")
        xn_ready = sem("xn_ready")
        res_ready = sem("res_ready")
        xT_done = sem("xT_done")
        xT_ready = sem("xT_ready")
        qk_done = sem("qk_done")
        qk_ready = sem("qk_ready")
        part1_ready = sem("part1_ready")
        rest_ready = sem("rest_ready")
        part2_ready = sem("part2_ready")
        part3_ready = sem("part3_ready")
        parts_out = sem("parts_out")
        stack_in = sem("stack_in")
        v_done = sem("v_done")
        v_ready = sem("v_ready")
        v_shift_in = sem("v_shift_in")
        scores_done = sem("scores_done")
        max_ready = sem("max_ready")
        exp_ready = sem("exp_ready")
        pT_done = sem("pT_done")
        pT_by_act = sem("pT_by_act")
        pT_by_dve = sem("pT_by_dve")
        pv_done = sem("pv_done")
        sum_step = sem("sum_step")
        weight_ready = sem("weight_ready")
        weightT_done = sem("weightT_done")
        weightT_ready = sem("weightT_ready")
        head_ready = sem("head_ready")
        ctx_zero = sem("ctx_zero")
        ctx_added = sem("ctx_added")
        wo_done = sem("wo_done")
        h2_ready = sem("h2_ready")
        h2_stored = sem("h2_stored")
        ln2_step = sem("ln2_step")
        rows0_ready = sem("rows0_ready")
        rows1_ready = sem("rows1_ready")
        x2T_done = sem("x2T_done")
        x2T_ready = sem("x2T_ready")
        gate_done = sem("gate_done")
        gate_ready = sem("gate_ready")
        logits_done = sem("logits_done")
        route_step = sem("route_step")
        taken_ready = sem("taken_ready")
        below_ready = sem("below_ready")
        score_e_ready = sem("score_e_ready")
        prefix_done = sem("prefix_done")
        place_step = sem("place_step")
        prefix_read = sem("prefix_read")
        token_step = sem("token_step")
        slots_ready = sem("slots_ready")
        payload_ready = sem("payload_ready")
        scattered = sem("scattered")

        pads_ready = sem("pads_ready")
        pads_in = sem("pads_in")
        tails_in = sem("tails_in")
        table_step = sem("table_step")
        table_ready = sem("table_ready")
        expert_weights_in = sem("expert_weights_in")
        slot_in = [sem(f"slot_in{i}") for i in range(RING)]
        gxT_done = sem("gxT_done")
        w1_done = sem("w1_done")
        gxT_ready = sem("gxT_ready")
        up_done = sem("up_done")
        silu_ready = sem("silu_ready")
        hid_ready = sem("hid_ready")
        hidT_done = sem("hidT_done")
        hidT_ready = sem("hidT_ready")
        y_done = sem("y_done")
        y_ready = sem("y_ready")
        y_added = sem("y_added")

        passed = sem("passed")

        block = ctx.enter_context(nc.Block())

        def wait_apart(eng, semaphore, value):
            eng.wait_ge(semaphore, value)
            if not isinstance(value, int):
                eng.sem_inc(passed, 1)

        def run_steps(eng, step):
            pairs = (B - 3) // 2
            for b in range(-2, 3):
                step(b, b % 2)
            with eng.Fori(1, pairs) as i:
                step(i * 2 + 1, 1)
                step(i * 2 + 2, 0)
            for b in range(2 * pairs + 1, B + 1):
                step(b, b % 2)

        def run_tiles(eng, step):
            for t in range(2 * RING):
                step(t, t % RING)
            with eng.Fori(2, MT // RING) as i:
                for r in range(RING):
                    step(i * RING + r, r)
            for t in range(MT // RING * RING, MT):
                step(t, t % RING)

        def later(t, n):
            return not isinstance(t, int) or t >= n

        def has(b):
            if not isinstance(b, int):
                return True, True, True, True
            return 0 <= b < B, 1 <= b <= B, 0 <= b + 1 < B, 0 <= b + 2 < B

        @block.sync
        def _(sp):
            def load_weights():
                for dst, src in ((wq_sb, Wq), (wk_sb, Wk), (wv_sb, Wv), (wo_sb, Wo)):
                    sp.dma_start(dst[:, :, :], src.rearrange("(c p) n -> p c n", p=P)).then_inc(weights_in, 16)
                sp.dma_start(gate_sb[:, :, :], gate_wT.rearrange("(c p) n -> p c n", p=P)).then_inc(weights_in, 16)
                for dst, src in ((bq_col, bq), (bk_col, bk)):
                    for c in range(C):
                        sp.dma_start(dst[:, c:c + 1], src[c * P:(c + 1) * P].rearrange("(p a) -> p a", a=1))\
                                .then_inc(weights_in, 16)
                sp.dma_start(bv_row[:, :], bv.partition_broadcast(P)).then_inc(weights_in, 16)
                sp.dma_start(bo_row[:, :], bo.partition_broadcast(P)).then_inc(weights_in, 16)
                sp.dma_start(inv_use[:, :], use).then_inc(weights_in, 16)

            sp.wait_ge(x_zeroed, 3)

            def step(b, par):
                att, tail, proj, inp = has(b)
                if inp:
                    b2 = b + 2
                    if not isinstance(b, int) or b2 >= 1:
                        wait_apart(sp, diffs_ready, b2 * 2)
                        wait_apart(sp, text_in, b2 * 16)
                    if isinstance(b, int):
                        img, txt = x[b2], x_txt[b2]
                    else:
                        img = x[bass.ds(b2, 1)].rearrange("a r c -> (a r) c")
                        txt = x_txt[bass.ds(b2, 1)].rearrange("a t -> (a t)")
                    sp.dma_start(x_here[:, :, 0:IMG], img.rearrange("(j p) c -> p j c", p=P)).then_inc(x_in, 16)
                    sp.dma_start(x_below[:, 0, 0:IMG], img[1:P + 1, :]).then_inc(x_in, 16)
                    sp.dma_start(x_below[0:112, 1, 0:IMG], img[P + 1:P + 113, :]).then_inc(x_in, 16)
                    sp.dma_start(x_below[112:127, 1, 0:IMG], img[P + 113:IMG, :]).then_inc(x_in, 16)
                    sp.dma_start(text_idx[0:TXT, :], txt.rearrange("(t a) -> t a", a=1)).then_inc(idx_in, 16)
                    if isinstance(b, int) and b2 == 0:
                        load_weights()
                def store_h2():
                    b0, hr = b - 1, h_res[1 - par]
                    wait_apart(sp, h2_ready, b0 * 2 + 2)
                    if isinstance(b, int):
                        dst = out[b0 * S:(b0 + 1) * S, :]
                    else:
                        dst = out[bass.ds(b0 * S, S), :]
                    sp.dma_start(dst[0:IMG, :].rearrange("(j p) n -> p j n", p=P), hr[:, 0:2, :]).then_inc(h2_stored, 16)
                    sp.dma_start(dst[IMG:S, :], hr[0:TXT, 2, :]).then_inc(h2_stored, 16)

                if isinstance(b, int) and b == -1:
                    sp.dma_start(nbias[:, :, :], pos_bias.rearrange("h q k -> q h k")).then_inc(bias_in, 16)
                if proj:
                    b1, par1 = b + 1, 1 - par
                    for n, (dst, slots) in enumerate([(q_stack[par1], Q_SLOTS), (k_stack[par1], K_SLOTS)]):
                        if n == 1 and tail:
                            store_h2()
                        wait_apart(sp, part3_ready, b1 * 2 + n + 1)
                        if n == 0 and (not isinstance(b, int) or b1 >= 1):
                            wait_apart(sp, stack_in, b1 * STACK_IN)
                        sp.dma_start(parts_dram[n].rearrange("(c p) t s -> p c t s", p=P),
                                     parts[:, 2 * n:2 * n + 2, :, :]).then_inc(parts_out, 16)
                        if n == 0 and (not isinstance(b, int) or b >= 1):
                            wait_apart(sp, scores_done, (b1 - 1) * G)
                        wait_apart(sp, parts_out, b1 * 32 + 16 * n + 16)
                        for s, part in enumerate(slots):
                            sp.dma_start(dst[s * HD:(s + 1) * HD, :, :],
                                         parts_dram[n, :, part, :].rearrange("(h d) s -> d h s", d=HD))\
                                .then_inc(stack_in, 16)
                        if n == 0:
                            vt = v_win[par1]
                            wait_apart(sp, v_ready, b1 * 3 + 3)
                            sp.dma_start(vt[0:64, 1, :], vt[64:128, 0, :]).then_inc(v_shift_in, 16)
                            sp.dma_start(vt[64:128, 1, :], vt[0:64, 2, :]).then_inc(v_shift_in, 16)
                            sp.dma_start(vt[0:64, 3, :], vt[64:128, 2, :]).then_inc(v_shift_in, 16)
                            o = STARTS[3] + 64 - STARTS[4]
                            sp.dma_start(vt[64:128, 3, :], vt[o:o + 64, 4, :]).then_inc(v_shift_in, 16)
                if tail and not proj:
                    store_h2()

            run_steps(sp, step)

            sp.wait_ge(scores_done, B * G)
            for e in range(E):
                sp.dma_start(w2_sb[:, e], w2[e].rearrange("(c p) n -> p c n", p=P)).then_inc(expert_weights_in, 16)
            sp.wait_ge(pads_ready, 1)
            for e in range(E):
                row = sp.value_load(region_end_i[0:1, e:e + 1], min_val=0, max_val=E * REGION)
                sp.dma_start(slots_dram[bass.ds(row, P), :], pad_rows[:, :]).then_inc(tails_in, 16)
            sp.wait_ge(pads_in, 16 * 2)
            sp.wait_ge(tails_in, 16 * E)
            sp.wait_ge(scattered, 96 * B)
            sp.wait_ge(table_ready, 1)

            sp.wait_ge(max_ready, B * G)
            def load_tile(t, r):
                row = sp.value_load(row_tab[0:1, bass.ds(t, 1)], min_val=0, max_val=E * REGION)
                if later(t, RING):
                    wait_apart(sp, y_added, (t - RING) * 16 + 16)
                sp.dma_start(g_rows[r], slots_dram[bass.ds(row, P), :]).then_inc(slot_in[r], 16)

            run_tiles(sp, load_tile)
            sp.wait_ge(h2_stored, 32 * B)

        @block.gpsimd
        def _(pool):
            pool.memset(x_here[:, :, :], 0.0).then_inc(x_zeroed, 1)
            pool.memset(x_below[:, :, :], 0.0).then_inc(x_zeroed, 1)
            pool.memset(text_idx[:, :], 0).then_inc(x_zeroed, 1)
            pool.memset(ident[:, :], 0.0).then_inc(const_set, 1)
            pool.memset(before[:, :], 1.0).then_inc(const_set, 1)
            pool.memset(ones[:, :], 1.0).then_inc(const_set, 1)
            pool.memset(text_ok[:, :], 1.0).then_inc(const_set, 1)
            pool.iota(expert_i[:, :], pattern=[[1, E]], base=0, channel_multiplier=0).then_inc(const_set, 1)
            pool.iota(lane_i[:, :], pattern=[[0, 1]], base=0, channel_multiplier=1).then_inc(const_set, 1)
            pool.iota(token_i[:, :], pattern=[[P, NT]], base=0, channel_multiplier=1).then_inc(const_set, 1)
            pool.iota(tile_i[:, :], pattern=[[1, MT]], base=0, channel_multiplier=0).then_inc(const_set, 1)
            pool.wait_ge(const_set, 8)
            pool.affine_select(out=ident[:, :], in_=ident[:, :], compare_op=ALU.not_equal, fill=1.0,
                               base=0, pattern=[[-1, P]], channel_multiplier=1).then_inc(const_set, 1)
            pool.affine_select(out=before[:, :], in_=before[:, :], compare_op=ALU.is_gt, fill=0.0,
                               base=0, pattern=[[1, P]], channel_multiplier=-1).then_inc(const_set, 1)
            pool.affine_select(out=text_ok[:, :], in_=text_ok[:, :], compare_op=ALU.is_gt, fill=0.0,
                               base=TXT, pattern=[[0, 1]], channel_multiplier=-1).then_inc(const_set, 1)
            pool.memset(h_in[:, :, :], 0.0).then_inc(zeroed, 1)
            pool.memset(v_all[:, :], 0.0).then_inc(zeroed, 1)
            pool.memset(pad_rows[:, 0:D + 1], 0.0).then_inc(zeroed, 1)
            pool.memset(rows[:, :, :, D:ROW], 0.0).then_inc(zeroed, 1)
            pool.wait_ge(zeroed, 4)
            pool.wait_ge(const2_set, 5)
            pool.dma_start(slots_dram[E * REGION:E * REGION + P, :], pad_rows[:, :]).then_inc(pads_in, 16)
            pool.dma_start(out[TOKENS:TOKENS + P, :], pad_rows[:, 0:D]).then_inc(pads_in, 16)
            NEWTON = 3
            ROOT = 2 + 4 * NEWTON

            def inverse_root(moments, rstd, chain, b, done):
                first = b * (ROOT - 1)
                pool.tensor_scalar(var_eps[:, :], moments[:, :, 1], EPS, None, ALU.add).then_inc(chain, 1)
                wait_apart(pool, chain, first + 1)
                pool.tensor_scalar(rstd[:, :].bitcast(I32), var_eps[:, :].bitcast(I32), -0.5, float(0x5F3759DF),
                                   ALU.mult, ALU.add).then_inc(chain, 1)
                for i in range(NEWTON):
                    pool.wait_ge(chain, first + 2 + 4 * i)
                    pool.tensor_tensor(root_tmp[:, :], rstd[:, :], rstd[:, :], ALU.mult).then_inc(chain, 1)
                    pool.wait_ge(chain, first + 3 + 4 * i)
                    pool.tensor_tensor(root_tmp[:, :], root_tmp[:, :], var_eps[:, :], ALU.mult).then_inc(chain, 1)
                    wait_apart(pool, chain, first + 4 + 4 * i)
                    pool.tensor_scalar(root_tmp[:, :], root_tmp[:, :], -0.5, 1.5, ALU.mult, ALU.add).then_inc(chain, 1)
                    pool.wait_ge(chain, first + 5 + 4 * i)
                    ins = pool.tensor_tensor(rstd[:, :], rstd[:, :], root_tmp[:, :], ALU.mult)
                    ins.then_inc(chain if i < NEWTON - 1 else done, 1)

            def step(b, par):
                att, tail, proj, inp = has(b)
                known = isinstance(b, int)
                for k in range(G):
                    if inp and k == 2:
                        b2 = b + 2
                        pool.wait_ge(x_in, b2 * 64 + 64)
                        if not known or b2 >= 1:
                            pool.wait_ge(image_ready, b2)
                        pool.tensor_tensor(diag[:, :, :], x_here[:, :, 0:IMG], x_below[:, :, 1:IMG + 1],
                                           ALU.subtract).then_inc(diffs_ready, 1)
                        pool.tensor_tensor(anti[:, :, :], x_below[:, :, 0:IMG], x_here[:, :, 1:IMG + 1],
                                           ALU.subtract).then_inc(diffs_ready, 1)
                    if proj and k in (6, 10):
                        n, b1 = (0, b + 1) if k == 6 else (1, b + 1)
                        pool.wait_ge(part2_ready, b1 * 2 + n + 1)
                        pool.tensor_tensor(parts[:, 2 * n:2 * n + 2, 2, :], rest[:, :, :],
                                           parts[:, 2 * n:2 * n + 2, 1, :], ALU.subtract).then_inc(part3_ready, 1)
                    if proj and k in (3, 6):
                        n, b1 = (0, b + 1) if k == 3 else (1, b + 1)
                        pool.wait_ge(part1_ready, b1 * 2 + n + 1)
                        if n == 1 or not known or b1 >= 1:
                            pool.wait_ge(part3_ready, b1 * 2 + n)
                        if n == 0 and (not known or b1 >= 3):
                            pool.wait_ge(gate_done, b1 - 2)
                        pool.tensor_tensor(rest[:, :, :], qk[:, 2 * n:2 * n + 2, :], parts[:, 2 * n:2 * n + 2, 0, :],
                                           ALU.subtract).then_inc(rest_ready, 1)
                    v = (k - 5) // NG
                    if (k - 5) % NG == 3 and ((att and v >= 0) or (tail and v < 0)):
                        wv = b * NW + v
                        w = v % NW
                        pool.wait_ge(head_ready, wv + 1)
                        pool.wait_ge(ctx_zero, b + 1 if v >= 0 else b)
                        if w > 0:
                            pool.wait_ge(ctx_added, wv)
                        view = ctxT[:, :, STARTS[w]:STARTS[w] + WIN]
                        pool.tensor_tensor(view, view, head_out[:, (par + v) % 2, :].rearrange("p (c q) -> p c q", c=C),
                                           ALU.add).then_inc(ctx_added, 1)
                    if att and k == 7:
                        if not known or b >= 1:
                            wait_apart(pool, wo_done, b * 2)
                        pool.memset(ctxT[:, :, :], 0.0).then_inc(ctx_zero, 1)
                    if proj and k == 12:
                        b1 = b + 1
                        if known and b1 == 0:
                            pool.wait_ge(weights_in, LOADS)
                        pool.wait_ge(image_ready, b1 + 1)
                        pool.wait_ge(text_in, b1 * 16 + 16)
                        if not known or b1 >= 2:
                            pool.wait_ge(h2_stored, (b1 - 1) * 32)
                            pool.wait_ge(rows0_ready, (b1 - 1) * 3)
                        pool.tensor_tensor(h_res[1 - par][:, :, :], h_in[:, :, :],
                                           bo_row[:, :].unsqueeze(1).to_broadcast([P, NT, D]), ALU.add)\
                            .then_inc(res_ready, 1)
                    if inp and k == 12:
                        b2 = b + 2
                        pool.wait_ge(idx_in, b2 * 16 + 16)
                        if not known or b2 >= 1:
                            pool.wait_ge(res_ready, b2)
                            wait_apart(pool, xn_ready, b2 * 3)
                        pool.indirect_dma_start(h_in[0:TXT, 2, :], None, table,
                                                bass.IndirectOffsetOnAxis(text_idx[0:TXT, 0:1], 0)).then_inc(text_in, 16)
                    if inp and k == 16:
                        if not known or b + 2 >= 1:
                            pool.wait_ge(xn_ready, b * 3 + 6)
                        wait_apart(pool, ln1_step, b * 6 + 18)
                        inverse_root(moments1, rstd1, root1_step, b + 2, rstd1_ready)
                    if tail and k == 9:
                        if not known or b >= 2:
                            pool.wait_ge(rows0_ready, b * 3 - 3)
                        wait_apart(pool, ln2_step, b * 6)
                        inverse_root(moments2, rstd2, root2_step, b - 1, rstd2_ready)
                    if tail and k == 13:
                        b0 = b - 1
                        pool.wait_ge(rows0_ready, b0 * 3 + 3)
                        if not known or b0 >= 1:
                            wait_apart(pool, scattered, b0 * 96)
                        pool.tensor_copy(rows[:, 1, :, 0:D], rows[:, 0, :, 0:D]).then_inc(rows1_ready, 1)
                    if tail and k == 19:
                        b0 = b - 1
                        pool.wait_ge(slots_ready, b0 + 1)
                        pool.wait_ge(payload_ready, b0 * 4 + 4)
                        wait_apart(pool, rows1_ready, b0 + 1)
                        for kk in range(K):
                            for j, (_, n) in enumerate(TILES):
                                pool.indirect_dma_start(slots_dram[:, :],
                                                        bass.IndirectOffsetOnAxis(slot_i[0:n, kk, j:j + 1], 0),
                                                        rows[0:n, kk, j, :], None).then_inc(scattered, 16)

            run_steps(pool, step)
            pool.wait_ge(h2_stored, 32 * B)

            def add_tile(t, r):
                pool.wait_ge(y_ready, t + 1)
                if later(t, 1):
                    wait_apart(pool, y_added, t * 16)
                pool.indirect_dma_start(out[:, :],
                                        bass.IndirectOffsetOnAxis(g_rows[r][:, D + 1:D + 2].bitcast(I32), 0),
                                        y_sb[r], None, compute_op=ALU.add).then_inc(y_added, 16)

            run_tiles(pool, add_tile)
            pool.wait_ge(y_added, 16 * MT)
            pool.wait_ge(pads_in, 16 * 2)

        @block.scalar
        def _(act):
            act.wait_ge(prep_done, 1)

            def step(b, par):
                att, tail, proj, inp = has(b)
                known = isinstance(b, int)
                for k in range(G):
                    if (k >= 1 and att) or (k < 1 and tail):
                        g = (k - 1) % NG
                        r = (k - 1) % 4
                        v = (k - 1) // NG
                        act.wait_ge(max_ready, b * G + k)
                        if g == 0 and (not known or b * NW + v >= 2):
                            act.wait_ge(sum_step, b * NW + v - 1)
                        for i, h in enumerate(group_heads(g)):
                            seg = probs[:, r, i * WIN:(i + 1) * WIN]
                            ins = act.activation(seg, seg, ACT.Exp, bias=neg_max[:, r, i:i + 1], scale=-1.0,
                                                 accum_out=row_sum[:, (par + v) % 2, h:h + 1])
                        ins.then_inc(exp_ready, 1)
                    if known and b == 0 and k >= 2 and k % 2 == 0 and k // 2 <= E:
                        e = k // 2 - 1
                        act.dma_start(w1_sb[:, e], w1[e].rearrange("(c p) n -> p c n", p=P)).then_inc(expert_weights_in, 16)
                        act.dma_start(w3_sb[:, e], w3[e].rearrange("(c p) n -> p c n", p=P)).then_inc(expert_weights_in, 16)
                    g = (k - 2) % NG
                    if g != 3 and ((k >= 2 and att) or (k < 2 and tail)):
                        n = b * G + (k - 2)
                        act.wait_ge(pT_done, n + 1)
                        if not known or n >= 2:
                            act.wait_ge(pv_done, n - 1)
                        act.activation(probsT[:, k % 2, :], t_bank[:, k % 2, :], ACT.Copy).then_inc(pT_by_act, 1)
                    v = (k - 4) // NG
                    if (k - 4) % NG == 3 and ((att and v >= 0) or (tail and v < 0)):
                        act.wait_ge(weightT_done, b * NW + v + 1)
                        if not known or b * NW + v >= 1:
                            act.wait_ge(head_ready, b * NW + v)
                        act.activation(weightT[:, :], o_bank[:, (par + v) % 2, C * WIN:2 * C * WIN], ACT.Copy)\
                            .then_inc(weightT_ready, 1)
                    if proj and k == 0:
                        b1 = b + 1
                        act.wait_ge(xT_done, b1 + 1)
                        if not known or b1 >= 1:
                            act.wait_ge(v_done, b1 * 2)
                        if not known or b1 >= 3:
                            act.wait_ge(logits_done, b1 - 2)
                        act.activation(xT[:, :, :], m_bank[:, :, 0:S], ACT.Copy).then_inc(xT_ready, 1)
                    if proj and k in (2, 4):
                        b1, n = b + 1, k // 2 - 1
                        for c in range(C):
                            act.wait_ge(qk_done, b1 * 4 + 2 * n + c + 1)
                            if not known or b1 >= 1:
                                act.wait_ge(rest_ready, b1 * 2)
                            act.activation(qk[:, 2 * n + c, :], m_bank[:, c, 0:S], ACT.Identity,
                                           bias=(bq_col if n == 0 else bk_col)[:, c:c + 1],
                                           scale=(-SCALE if n == 0 else 1.0)).then_inc(qk_ready, 1)
                    if tail and k == 12:
                        act.wait_ge(x2T_done, b)
                        if proj:
                            act.wait_ge(part3_ready, b * 2 + 4)
                        act.activation(x2T[:, :, :], m_bank[:, :, 0:S], ACT.Copy).then_inc(x2T_ready, 1)
                    if tail and k == 14:
                        act.wait_ge(gate_done, b)
                        if proj:
                            act.wait_ge(v_done, b * 2 + 4)
                        act.activation(gateT, m_bank[0:E, 0, 0:S], ACT.Copy).then_inc(gate_ready, 1)
                    if tail and k == 17:
                        act.wait_ge(below_ready, b)
                        if not known or b >= 2:
                            act.wait_ge(payload_ready, (b - 1) * 4)
                        act.activation(score_e[:, :, :], below_best[:, :, :], ACT.Exp).then_inc(score_e_ready, 1)

            run_steps(act, step)

            def gxT_tile(t, par):
                act.wait_ge(gxT_done, t + 1)
                if later(t, 2):
                    act.wait_ge(up_done, t - 1)
                act.activation(gxT[par], m_bank[:, 0, 0:D], ACT.Copy).then_inc(gxT_ready, 1)

            def tile_step(t, r):
                act.wait_ge(w1_done, t + 1)
                if later(t, 2):
                    act.wait_ge(hidT_done, t - 1)
                act.activation(hid[r % 2], s_bank[:, r % 2, :], ACT.Silu).then_inc(silu_ready, 1)
                if not isinstance(t, int) or t + 1 < MT:
                    gxT_tile(t + 1, 1 - r % 2)

            gxT_tile(0, 0)
            run_tiles(act, tile_step)

        @block.vector
        def _(dve):
            for bank in (s_bank, t_bank, o_bank, m_bank):
                dve.memset(bank[:, :, :], 0.0).then_inc(psum_zeroed, 1)
            dve.wait_ge(const_set, 11)
            dve.tensor_copy(expert_no[:, :], expert_i[:, :]).then_inc(const2_set, 1)
            dve.tensor_copy(token_f[:, :], token_i[:, :]).then_inc(const2_set, 1)
            dve.tensor_scalar(pad_rows[:, D + 1:D + 2].bitcast(I32), lane_i[:, :], float(TOKENS), None, ALU.add)\
                .then_inc(const2_set, 1)
            dve.tensor_scalar(region_end[:, :], expert_i[:, :], float(REGION), None, ALU.mult).then_inc(const2_set, 1)
            dve.tensor_copy(lane[:, :], lane_i[:, :]).then_inc(const2_set, 1)
            dve.wait_ge(const2_set, 5)
            dve.wait_ge(zeroed, 4)

            def moments_of(src, stats, moments, b, chain):
                for j in range(NT):
                    dve.bn_stats(stats[:, j, :], src[:, j, :]).then_inc(chain, 1)
                for j in range(NT):
                    wait_apart(dve, chain, b * 6 + 1 + j)
                    dve.bn_aggr(moments[:, j, :], stats[:, j, :]).then_inc(chain, 1)

            def normalise(src, moments, rstd, dst, done):
                for j in range(NT):
                    dve.tensor_scalar(dst(j), src[:, j, :], moments[:, j, 0:1], rstd[:, j:j + 1],
                                      ALU.subtract, ALU.mult).then_inc(done, 1)

            RS = 8
            PS = 3

            def step(b, par):
                att, tail, proj, inp = has(b)
                known = isinstance(b, int)
                if known and b == -1:
                    dve.wait_ge(weights_in, LOADS)
                    dve.tensor_scalar(bq_col[:, :], bq_col[:, :], -SCALE, None, ALU.mult).then_inc(prep_done, 1)
                if known and b == 0:
                    dve.wait_ge(bias_in, 16)
                    dve.tensor_scalar(nbias[:, :, :], nbias[:, :, :], -1.0, None, ALU.mult).then_inc(prep_done, 1)
                    dve.wait_ge(prep_done, 2)
                for k in range(G):
                    if att:
                        g, r = k % NG, k % 4
                        dve.wait_ge(scores_done, b * G + k + 1)
                        if not known or b * G + k >= 4:
                            wait_apart(dve, pT_done, b * G + k - 3)
                        for i, h in enumerate(group_heads(g)):
                            ins = dve.tensor_tensor_reduce(probs[:, r, i * WIN:(i + 1) * WIN],
                                                           s_bank[:, k % 2, i * WIN:(i + 1) * WIN], nbias[:, h, :],
                                                           1.0, BIG, ALU.add, ALU.min, neg_max[:, r, i:i + 1])
                        ins.then_inc(max_ready, 1)
                    v = (k - 2) // NG
                    if (k - 2) % NG == 3 and ((att and v >= 0) or (tail and v < 0)):
                        n = b * G + (k - 2)
                        wv, vp = b * NW + v, (par + v) % 2
                        dve.wait_ge(exp_ready, n + 1)
                        dve.reciprocal(inv_sum[:, vp, :], row_sum[:, vp, :]).then_inc(sum_step, 1)
                        dve.wait_ge(pT_done, n + 1)
                        if not known or n >= 2:
                            dve.wait_ge(pv_done, n - 1)
                        dve.tensor_copy(probsT[:, k % 2, :], t_bank[:, k % 2, :]).then_inc(pT_by_dve, 1)
                        dve.wait_ge(sum_step, wv + 1)
                        if not known or wv >= 2:
                            dve.wait_ge(weightT_done, wv - 1)
                        dve.tensor_scalar(weight[:, vp, :, :], inv_sum[:, vp, :].unsqueeze(2).to_broadcast([P, H, HD]),
                                          inv_use[:, v % NW:v % NW + 1], None, ALU.mult).then_inc(weight_ready, 1)
                    v = (k - 5) // NG
                    if (k - 5) % NG == 3 and ((att and v >= 0) or (tail and v < 0)):
                        wv, vp = b * NW + v, (par + v) % 2
                        dve.wait_ge(weightT_ready, wv + 1)
                        if not known or wv >= 2:
                            dve.wait_ge(ctx_added, wv - 1)
                        dve.tensor_tensor(head_out[:, vp, :], o_bank[:, vp, 0:C * WIN], weightT[:, :], ALU.mult)\
                            .then_inc(head_ready, 1)
                    if proj and k in (3, 5):
                        n, b1 = (k - 3) // 2, b + 1
                        dve.wait_ge(qk_ready, b1 * 4 + 2 * n + 2)
                        if not known or b1 >= 1:
                            dve.wait_ge(parts_out, b1 * 32)
                        dve.tensor_copy(parts[:, 2 * n:2 * n + 2, 0, :], qk[:, 2 * n:2 * n + 2, :])\
                            .then_inc(part1_ready, 1)
                    if proj and k in (6, 10):
                        n, b1 = (0, b + 1) if k == 6 else (1, b + 1)
                        dve.wait_ge(rest_ready, b1 * 2 + n + 1)
                        dve.tensor_copy(parts[:, 2 * n:2 * n + 2, 1, :], rest[:, :, :]).then_inc(part2_ready, 1)
                    if proj and k == 6:
                        b1, vt = b + 1, v_win[1 - par]
                        if not known or b1 >= 2:
                            dve.wait_ge(pv_done, (b1 - 1) * G)
                        for n, w in enumerate((0, 2, 4)):
                            dve.wait_ge(v_done, b1 * 2 + 1 + n // 2)
                            cols = vt[:, w, :].rearrange("p (t a e) -> p t a e", a=3, e=HD)[:, :, 0:3:2, :]
                            src = m_bank[:, n // 2, (n % 2) * D:(n % 2) * D + D]
                            dve.tensor_tensor(cols, src.rearrange("p (t a e) -> p t a e", a=2, e=HD),
                                              bv_row[:, :].rearrange("p (t a e) -> p t a e", a=2, e=HD),
                                              ALU.add).then_inc(v_ready, 1)
                    if tail and k == 8:
                        b0, hr = b - 1, h_res[1 - par]
                        dve.wait_ge(wo_done, b0 * 2 + 1)
                        dve.wait_ge(res_ready, b0 + 1)
                        dve.tensor_tensor(hr[:, 0:2, :], m_bank[:, 0, :].rearrange("p (j n) -> p j n", j=2),
                                          hr[:, 0:2, :], ALU.add).then_inc(h2_ready, 1)
                        dve.wait_ge(wo_done, b0 * 2 + 2)
                        dve.tensor_tensor(hr[0:TXT, 2, :], m_bank[0:TXT, 1, 0:D], hr[0:TXT, 2, :], ALU.add)\
                            .then_inc(h2_ready, 1)
                    if tail and k == 8:
                        b0, hr = b - 1, h_res[1 - par]
                        dve.wait_ge(h2_ready, b0 * 2 + 2)
                        if not known or b0 >= 1:
                            dve.wait_ge(rows0_ready, b0 * 3)
                            dve.wait_ge(rstd2_ready, b0)
                        moments_of(hr, stats2, moments2, b0, ln2_step)
                    if tail and k == 11:
                        b0, hr = b - 1, h_res[1 - par]
                        dve.wait_ge(rstd2_ready, b0 + 1)
                        if not known or b0 >= 1:
                            dve.wait_ge(scattered, b0 * 96)
                            dve.wait_ge(x2T_done, b0)
                        normalise(hr, moments2, rstd2, lambda j: rows[:, 0, j, 0:D], rows0_ready)
                    if tail and k == 16:
                        b0 = b - 1
                        dve.wait_ge(logits_done, b0 + 1)
                        dve.tensor_copy(logits[:, :, :], m_bank[:, 1, 0:NT * E].rearrange("p (j e) -> p j e", j=NT))\
                            .then_inc(route_step, 1)
                        wait_apart(dve, route_step, b0 * RS + 1)
                        for j in range(NT):
                            dve.max(best[:, j, :], logits[:, j, :]).then_inc(route_step, 1)
                        for j in range(NT):
                            wait_apart(dve, route_step, b0 * RS + 2 + j)
                            dve.max_index(best_i[:, j, :], best[:, j, :], logits[:, j, :]).then_inc(route_step, 1)
                        if not known or b0 >= 1:
                            dve.wait_ge(score_e_ready, b0)
                        dve.tensor_tensor(below_best[:, :, :], best[:, :, :],
                                          best[:, :, 0:1].to_broadcast([P, NT, E]), ALU.subtract)\
                            .then_inc(below_ready, 1)
                        dve.wait_ge(route_step, b0 * RS + 7)
                        dve.tensor_copy(pick[:, :, :], best_i[:, :, 0:K]).then_inc(route_step, 1)
                    if tail and k == 17:
                        b0 = b - 1
                        dve.wait_ge(route_step, b0 * RS + 8)
                        for kk in range(K):
                            dve.tensor_tensor(onehot[:, kk, :, :],
                                              expert_no[:, :].unsqueeze(1).to_broadcast([P, NT, E]),
                                              pick[:, :, kk:kk + 1].to_broadcast([P, NT, E]), ALU.is_equal)\
                                .then_inc(place_step, 1)
                        dve.wait_ge(place_step, b0 * PS + 2)
                        dve.tensor_scalar(onehot[:, :, 2, :], onehot[:, :, 2, :], text_ok[:, 0:1], None, ALU.mult)\
                            .then_inc(place_step, 1)
                        dve.wait_ge(place_step, b0 * PS + 3)
                        dve.tensor_tensor(taken[:, :, :], onehot[:, 0, :, :], onehot[:, 1, :, :], ALU.add)\
                            .then_inc(taken_ready, 1)
                    if tail and k == 18:
                        b0 = b - 1
                        dve.wait_ge(score_e_ready, b0 + 1)
                        dve.tensor_reduce(score_sum[:, :], score_e[:, :, :], AX.X, ALU.add).then_inc(payload_ready, 1)
                        dve.wait_ge(payload_ready, b0 * 4 + 1)
                        dve.reciprocal(score_inv[:, :], score_sum[:, :]).then_inc(payload_ready, 1)
                        dve.wait_ge(payload_ready, b0 * 4 + 2)
                        dve.tensor_tensor(rows[:, :, :, D].rearrange("p k j -> p j k"), score_e[:, :, 0:K],
                                          score_inv[:, :].unsqueeze(2).to_broadcast([P, NT, K]), ALU.mult)\
                            .then_inc(payload_ready, 1)
                        dve.tensor_copy(rows[:, :, :, D + 1].bitcast(I32),
                                        token_f[:, :].unsqueeze(1).to_broadcast([P, K, NT])).then_inc(payload_ready, 1)
                        dve.wait_ge(payload_ready, b0 * 4 + 4)
                        dve.tensor_scalar(token_f[:, :], token_f[:, :], float(S), None, ALU.add).then_inc(token_step, 1)
                    if tail and k == 19:
                        b0 = b - 1
                        dve.wait_ge(prefix_done, b0 + 1)
                        dve.tensor_tensor(place[:, :, :], m_bank[:, 0, 0:NT * E].rearrange("p (j e) -> p j e", j=NT),
                                          region_end[:, :].unsqueeze(1).to_broadcast([P, NT, E]), ALU.add)\
                            .then_inc(prefix_read, 1)
                        dve.wait_ge(prefix_read, b0 * 4 + 1)
                        dve.tensor_tensor(region_end[:, :], region_end[:, :], m_bank[:, 0, NT * E:(NT + 1) * E], ALU.add)\
                            .then_inc(prefix_read, 1)
                        dve.tensor_tensor(place_k[:, :, :, :], onehot[:, :, :, :],
                                          place[:, :, :].unsqueeze(1).to_broadcast([P, K, NT, E]), ALU.mult)\
                            .then_inc(prefix_read, 1)
                        dve.wait_ge(prefix_read, b0 * 4 + 3)
                        dve.tensor_reduce(slot_f[:, :, :], place_k[:, :, :, :], AX.X, ALU.add).then_inc(prefix_read, 1)
                        dve.wait_ge(prefix_read, b0 * 4 + 4)
                        dve.tensor_copy(slot_i[:, :, :], slot_f[:, :, :]).then_inc(slots_ready, 1)
                    if inp and k == 4:
                        b2 = b + 2
                        for n, d in enumerate((diag, anti)):
                            bits = d[:, :, :].bitcast(I32)
                            dve.wait_ge(diffs_ready, b2 * 2 + n + 1)
                            dve.tensor_scalar(bits, bits, 0x7FFFFFFF, None, ALU.bitwise_and).then_inc(conv_step, 1)
                    if inp and k == 12:
                        b2 = b + 2
                        dve.wait_ge(conv_step, b2 * 3 + 2)
                        dve.tensor_tensor(diag[:, :, :], diag[:, :, :], anti[:, :, :], ALU.add).then_inc(conv_step, 1)
                    if inp and k == 14:
                        b2 = b + 2
                        dve.wait_ge(conv_step, b2 * 3 + 3)
                        if not known or b2 >= 1:
                            dve.wait_ge(res_ready, b2)
                            dve.wait_ge(xn_ready, b2 * 3)
                        dve.tensor_scalar(h_in[:, 0:2, :], diag[:, :, :], 1.0, 0.0, ALU.min, ALU.max)\
                            .then_inc(image_ready, 1)
                    if inp and k == 15:
                        b2 = b + 2
                        dve.wait_ge(image_ready, b2 + 1)
                        dve.wait_ge(text_in, b2 * 16 + 16)
                        if not known or b2 >= 1:
                            dve.wait_ge(rstd1_ready, b2)
                        moments_of(h_in, stats1, moments1, b2, ln1_step)
                    if inp and k == 18:
                        b2 = b + 2
                        dve.wait_ge(rstd1_ready, b2 + 1)
                        if not known or b2 >= 1:
                            dve.wait_ge(xT_done, b2)
                        normalise(h_in, moments1, rstd1, lambda j: xn[:, j, :], xn_ready)

            run_steps(dve, step)

            steps = [0]

            def link(ins):
                steps[0] += 1
                ins.then_inc(table_step, 1)
                dve.wait_ge(table_step, steps[0])

            dve.wait_ge(prefix_read, B * 4)
            dve.tensor_copy(region_end_i[:, :], region_end[:, :]).then_inc(pads_ready, 1)
            dve.wait_ge(rest_ready, 2 * B)
            link(dve.tensor_copy(tile_no, tile_i[:, :]))
            link(dve.tensor_scalar(tile_base[:, :], expert_no[:, :], float(REGION), None, ALU.mult))
            link(dve.tensor_tensor(n_rows[:, :], region_end[:, :], tile_base[:, :], ALU.subtract))
            link(dve.tensor_scalar(n_rows[:, :], n_rows[:, :], float(P - 1), None, ALU.add))
            link(dve.tensor_copy(n_rows_i[:, :], n_rows[:, :]))
            link(dve.tensor_scalar(n_rows_i[:, :], n_rows_i[:, :], P.bit_length() - 1, None, ALU.logical_shift_right))
            link(dve.tensor_copy(n_tiles[:, :], n_rows_i[:, :]))
            link(dve.tensor_copy(tiles_to[:, 0:1], n_tiles[:, 0:1]))
            for e in range(1, E):
                link(dve.tensor_tensor(tiles_to[:, e:e + 1], tiles_to[:, e - 1:e], n_tiles[:, e:e + 1], ALU.add))
            link(dve.tensor_tensor(tab_ge, tile_no.unsqueeze(2).to_broadcast([P, MT, E]),
                                   tiles_to[:, :].unsqueeze(1).to_broadcast([P, MT, E]), ALU.is_ge))
            link(dve.tensor_reduce(tab_e, tab_ge, AX.X, ALU.add))
            link(dve.tensor_tensor(tab_ge, tab_ge, n_tiles[:, :].unsqueeze(1).to_broadcast([P, MT, E]), ALU.mult))
            link(dve.tensor_reduce(tab_b, tab_ge, AX.X, ALU.add))
            link(dve.tensor_tensor(tab_b, tile_no, tab_b, ALU.subtract))
            link(dve.tensor_scalar(tab_b, tab_b, float(P), None, ALU.mult))
            link(dve.scalar_tensor_tensor(out=tab_b, in0=tab_e, scalar=float(REGION), in1=tab_b,
                                          op0=ALU.mult, op1=ALU.add))
            link(dve.tensor_scalar(tab_b, tab_b, float(E * REGION), None, ALU.min))
            link(dve.tensor_copy(row_tab, tab_b))
            link(dve.tensor_scalar(tab_e, tab_e, float(E - 1), None, ALU.min))
            dve.tensor_copy(exp_tab, tab_e).then_inc(table_ready, 1)

            def y_tile(t, r):
                dve.wait_ge(y_done, t + 1)
                if later(t, RING):
                    dve.wait_ge(y_added, (t - RING) * 16 + 16)
                dve.wait_ge(slot_in[r], (t - r) * (16 // RING) + 16)
                dve.tensor_scalar(y_sb[r], o_bank[:, 1, 0:D], g_rows[r][:, D:D + 1], None, ALU.mult)\
                    .then_inc(y_ready, 1)

            def tile_step(t, r):
                dve.wait_ge(silu_ready, t + 1)
                dve.wait_ge(up_done, t + 1)
                dve.tensor_tensor(hid[r % 2], hid[r % 2], t_bank[:, r % 2, :], ALU.mult).then_inc(hid_ready, 1)
                if later(t, 1):
                    y_tile(t - 1, (r - 1) % RING)
                dve.wait_ge(hidT_done, t + 1)
                if later(t, 2):
                    dve.wait_ge(y_done, t - 1)
                dve.tensor_copy(hidT[r % 2], o_bank[:, 0, :]).then_inc(hidT_ready, 1)

            dve.wait_ge(pT_done, B * G)
            run_tiles(dve, tile_step)
            y_tile(MT - 1, (MT - 1) % RING)

        @block.tensor
        def _(pe):
            pe.wait_ge(psum_zeroed, 4)
            pe.wait_ge(const_set, 11)
            pe.wait_ge(weights_in, LOADS)

            def step(b, par):
                att, tail, proj, inp = has(b)
                known = isinstance(b, int)
                for k in range(G):
                    if att:
                        n, g, w = b * G + k, k % NG, k // NG
                        if k == 0:
                            pe.wait_ge(stack_in, b * STACK_IN + STACK_IN)
                        if not known or n >= 2:
                            pe.wait_ge(max_ready, n - 1)
                        lo = STARTS[w]
                        for i, h in enumerate(group_heads(g)):
                            mm = pe.matmul(s_bank[:, k % 2, i * WIN:(i + 1) * WIN],
                                           q_stack[par][0:KROWS, h, lo:lo + WIN], k_stack[par][0:KROWS, h, lo:lo + WIN],
                                           start=True, stop=True)
                        mm.then_inc(scores_done, 1)
                    if (k >= 3 and att) or (k < 3 and tail):
                        n, r = b * G + (k - 3), (k - 3) % 4
                        pe.wait_ge(exp_ready, n + 1)
                        if not known or n >= 2:
                            if (k - 5) % NG == 3:
                                pe.wait_ge(pT_by_dve, b * NW + (k - 5) // NG + 1)
                            else:
                                pe.wait_ge(pT_by_act, (b * NW + (k - 5) // NG) * 3 + (k - 5) % NG + 1)
                        for i in range(GH):
                            mm = pe.transpose(t_bank[:, (k - 3) % 2, i * WIN:(i + 1) * WIN],
                                              probs[:, r, i * WIN:(i + 1) * WIN], ident[:, :])
                        mm.then_inc(pT_done, 1)
                    if (k >= 4 and att) or (k < 4 and tail):
                        m, n = k - 4, b * G + (k - 4)
                        w, g = (m // NG) % NW, m % NG
                        vp, bp = (par + m // NG) % 2, par if m >= 0 else 1 - par
                        if g == 3:
                            pe.wait_ge(pT_by_dve, b * NW + m // NG + 1)
                        else:
                            pe.wait_ge(pT_by_act, (b * NW + m // NG) * 3 + g + 1)
                        if m == 0:
                            pe.wait_ge(v_ready, b * 3 + 3)
                            pe.wait_ge(v_shift_in, b * 64 + 64)
                        if g == 0 and (not known or b * NW + m // NG >= 2):
                            pe.wait_ge(head_ready, b * NW + m // NG - 1)
                        for i, h in enumerate(group_heads(g)):
                            c0 = (h // 2) * VW + (h % 2) * HD
                            mm = pe.matmul(o_bank[32 * i:32 * i + 32, vp, (g // 2) * WIN:(g // 2 + 1) * WIN],
                                           v_win[bp][:, w, c0:c0 + 2 * HD],
                                           probsT[:, (k - 4) % 2, i * WIN:(i + 1) * WIN],
                                           start=(g % 2 == 0), stop=(g % 2 == 1), skip_group_check=True)
                        mm.then_inc(pv_done, 1)
                        if g == 3:
                            pe.wait_ge(weight_ready, b * NW + m // NG + 1)
                            for c in range(C):
                                mm = pe.transpose(o_bank[:, vp, (C + c) * WIN:(C + c + 1) * WIN],
                                                  weight[:, vp, 8 * c:8 * c + 8, :].rearrange("p h d -> p (h d)"),
                                                  ident[:, :])
                            mm.then_inc(weightT_done, 1)
                    b1 = b + 1
                    if proj and k == 1:
                        pe.wait_ge(xn_ready, b1 * 3 + 3)
                        if not known or b1 >= 3:
                            pe.wait_ge(prefix_read, (b1 - 2) * 4)
                            pe.wait_ge(route_step, (b1 - 2) * 8)
                        for c in range(C):
                            for j, (t0, n) in enumerate(TILES):
                                mm = pe.transpose(m_bank[:, c, t0:t0 + n], xn[0:n, j, c * P:(c + 1) * P], ident[0:n, 0:n])
                        mm.then_inc(xT_done, 1)
                    if proj and k in (2, 4):
                        n = k // 2 - 1
                        wt = wq_sb if n == 0 else wk_sb
                        for c in range(C):
                            if n == 0:
                                pe.wait_ge(xT_ready, b1 + 1)
                            else:
                                pe.wait_ge(qk_ready, b1 * 4 + c + 1)
                            for a in range(C):
                                mm = pe.matmul(m_bank[:, c, 0:S], wt[:, a, c * P:(c + 1) * P], xT[:, a, :],
                                               start=(a == 0), stop=(a == C - 1))
                            mm.then_inc(qk_done, 1)
                    if proj and k == 6:
                        for bank, o, w in ((0, 0, 0), (0, D, 2), (1, 0, 4)):
                            pe.wait_ge(qk_ready, b1 * 4 + 3 + bank)
                            for a in range(C):
                                mm = pe.matmul(m_bank[:, bank, o:o + D], xT[:, a, STARTS[w]:STARTS[w] + WIN],
                                               wv_sb[:, a, :], start=(a == 0), stop=(a == C - 1))
                            if w:
                                mm.then_inc(v_done, 1)
                    b0 = b - 1
                    if tail and k == 8:
                        pe.wait_ge(ctx_added, b0 * NW + NW)
                        if proj:
                            pe.wait_ge(v_ready, b1 * 3 + 3)
                        elif b0 >= 1:
                            pe.wait_ge(prefix_read, b0 * 4)
                            pe.wait_ge(route_step, b0 * 8)
                        for j, (t0, n) in enumerate(TILES):
                            for a in range(C):
                                mm = pe.matmul(m_bank[0:n, j // 2, (j % 2) * D:(j % 2) * D + D], ctxT[:, a, t0:t0 + n],
                                               wo_sb[:, a, :], start=(a == 0), stop=(a == C - 1))
                            if j:
                                mm.then_inc(wo_done, 1)
                    if tail and k == 12:
                        pe.wait_ge(rows0_ready, b0 * 3 + 3)
                        pe.wait_ge(h2_ready, b0 * 2 + 2)
                        for c in range(C):
                            for j, (t0, n) in enumerate(TILES):
                                mm = pe.transpose(m_bank[:, c, t0:t0 + n], rows[0:n, 0, j, c * P:(c + 1) * P],
                                                  ident[0:n, 0:n])
                        mm.then_inc(x2T_done, 1)
                    if tail and k == 14:
                        pe.wait_ge(x2T_ready, b0 + 1)
                        for a in range(C):
                            mm = pe.matmul(m_bank[0:E, 0, 0:S], gate_sb[:, a, :], x2T[:, a, :],
                                           start=(a == 0), stop=(a == C - 1))
                        mm.then_inc(gate_done, 1)
                    if tail and k == 16:
                        wait_apart(pe, gate_ready, b0 + 1)
                        for j, (t0, n) in enumerate(TILES):
                            mm = pe.transpose(m_bank[0:n, 1, j * E:(j + 1) * E], gateT[:, t0:t0 + n], ident[0:E, 0:E])
                        mm.then_inc(logits_done, 1)
                    if tail and k == 19:
                        pe.wait_ge(taken_ready, b0 + 1)
                        pe.matmul(m_bank[:, 0, 0:NT * E], before[:, :], taken[:, :, :].rearrange("p j e -> p (j e)"),
                                  start=True, stop=False, skip_group_check=True)
                        for j in range(NT):
                            mm = pe.matmul(m_bank[:, 0, (j + 1) * E:(NT + 1) * E].rearrange("p (r e) -> p r e", e=E),
                                           ones[:, :], taken[:, j:j + 1, :].to_broadcast([P, NT - j, E]),
                                           start=False, stop=(j == NT - 1), skip_group_check=True)
                        mm.then_inc(prefix_done, 1)

            run_steps(pe, step)

            pe.wait_ge(expert_weights_in, 16 * 3 * E)
            pe.wait_ge(table_ready, 1)

            def gx_tile(t, r):
                pe.wait_ge(slot_in[r], (t - r) * (16 // RING) + 16)
                if later(t, 1):
                    pe.wait_ge(gxT_ready, t)
                for c in range(C):
                    mm = pe.transpose(m_bank[:, 0, c * P:(c + 1) * P], g_rows[r][:, c * P:(c + 1) * P], ident[:, :])
                mm.then_inc(gxT_done, 1)

            def up_tile(t, par):
                e = pe.value_load(exp_tab[0:1, bass.ds(t, 1)], min_val=0, max_val=E - 1)
                pe.wait_ge(gxT_ready, t + 1)
                if later(t, 2):
                    pe.wait_ge(hid_ready, t - 1)
                for bank, wt, done in ((s_bank, w1_sb, w1_done), (t_bank, w3_sb, up_done)):
                    for a in range(C):
                        mm = pe.matmul(bank[:, par, :], gxT[par][:, a * P:(a + 1) * P],
                                       wt[:, bass.ds(e, 1), a, :].rearrange("p o n -> p (o n)"),
                                       start=(a == 0), stop=(a == C - 1))
                    mm.then_inc(done, 1)

            def tile_step(t, r):
                pe.wait_ge(hid_ready, t + 1)
                if later(t, 1):
                    pe.wait_ge(hidT_ready, t)
                for a in range(HC):
                    mm = pe.transpose(o_bank[:, 0, a * P:(a + 1) * P], hid[r % 2][:, a * P:(a + 1) * P], ident[:, :])
                mm.then_inc(hidT_done, 1)
                if not isinstance(t, int) or t + 1 < MT:
                    up_tile(t + 1, (r + 1) % 2)
                if not isinstance(t, int) or t + 2 < MT:
                    gx_tile(t + 2, (r + 2) % RING)
                e = pe.value_load(exp_tab[0:1, bass.ds(t, 1)], min_val=0, max_val=E - 1)
                pe.wait_ge(hidT_ready, t + 1)
                if later(t, 1):
                    pe.wait_ge(y_ready, t)
                for a in range(HC):
                    mm = pe.matmul(o_bank[:, 1, 0:D], hidT[r % 2][:, a * P:(a + 1) * P],
                                   w2_sb[:, bass.ds(e, 1), a, :].rearrange("p o n -> p (o n)"),
                                   start=(a == 0), stop=(a == HC - 1))
                mm.then_inc(y_done, 1)

            gx_tile(0, 0)
            up_tile(0, 0)
            gx_tile(1, 1)
            run_tiles(pe, tile_step)


_INS = ["x", "x_txt", "L0_txt_weight", "L0_attn_Wq", "L0_attn_bq", "L0_attn_Wk", "L0_attn_bk", "L0_attn_Wv",
        "L0_attn_bv", "L0_attn_Wo", "L0_attn_bo", "L0_attn_pos_bias", "L0_ffn_gate_w", "L0_ffn_w1", "L0_ffn_w2",
        "L0_ffn_w3"]


def kernel(**inputs):
    import numpy as _np
    import concourse.bacc as _bacc
    from concourse import mybir as _mybir
    from concourse.bass_utils import run_bass_kernel_spmd as _run

    nc = _bacc.Bacc("TRN2", target_bir_lowering=False, num_devices=1)
    arrays, args = {}, []
    for name in _INS:
        a = _np.asarray(inputs[name])
        if name == "x":
            a = a.reshape(B, IMG, D)
        if name == "L0_ffn_gate_w":
            a = a.T
        a = _np.ascontiguousarray(a)
        arrays[f"in_{name}_dram"] = a
        args.append(nc.dram_tensor(f"in_{name}_dram", a.shape, _mybir.dt.from_np(a.dtype), kind="ExternalInput").ap())
    counts = _np.zeros((P, NW), _np.float32)
    for w, lo in enumerate(STARTS):
        for q in range(WIN):
            counts[q, w] = 1.0 / sum(s <= lo + q < s + WIN for s in STARTS)
    arrays["counts_dram"] = counts
    args.append(nc.dram_tensor("counts_dram", counts.shape, _mybir.dt.from_np(counts.dtype), kind="ExternalInput").ap())
    args.append(nc.dram_tensor("out_dram", (TOKENS + P, D), _mybir.dt.float32, kind="ExternalOutput").ap())
    build(nc, *args)
    r = _run(nc, [arrays], core_ids=[0])
    return r.results[0]["out_dram"][:TOKENS].reshape(B, S, D)
```
